# Optimizing a Trainium2 kernel written in Bass

```python
import numpy as np
import jax
import jax.numpy as jnp

def _softmax(x, axis=-1):
    return jax.nn.softmax(x, axis=axis)

def _gelu(x):
    return jax.nn.gelu(x, approximate=True)

def _silu(x):
    return jax.nn.silu(x)

def _sigmoid(x):
    return jax.nn.sigmoid(x)

def _layernorm(x, axis=-1, eps=1e-05):
    m = jnp.mean(x, axis=axis, keepdims=True)
    v = jnp.var(x, axis=axis, keepdims=True)
    return (x - m) / jnp.sqrt(v + eps)

def _scatter_add(tgt, idx, src, axis=0):
    return tgt.at[idx].add(src)

def _segment_sum(src, seg, n):
    return jax.ops.segment_sum(src, seg, n)
kernel_name = 'mk_gnn_preln_d4_gnn_r32_7ebf1a'

def setup_inputs(seed: int=0):
    np.random.seed(seed)
    _w = jnp.asarray

    def _rec_inputs():
        import jax
        import jax.numpy as jnp
        _gk = jax.random.key(seed)
        x = -0.0003713 + 1 * jax.random.normal(jax.random.fold_in(_gk, 1), (3125, 256), jnp.float32)
        src = jax.random.randint(jax.random.fold_in(_gk, 2), (50000,), 0, 3125, jnp.int32)
        dst = jax.random.randint(jax.random.fold_in(_gk, 3), (50000,), 0, 3125, jnp.int32)
        _o = jnp.argsort(dst, stable=True)
        src = src[_o]
        dst = dst[_o]
        edge_attr_64 = 5.96457e-05 + 0.999887 * jax.random.normal(jax.random.fold_in(_gk, 12), (50000, 64), jnp.float32)
        node_vec1 = jax.random.uniform(jax.random.fold_in(_gk, 14), (3125, 1), jnp.float32, 0.0, 0.999943)
        return (x, src, dst, edge_attr_64, node_vec1)
    x, src, dst, edge_attr_64, node_vec1 = _rec_inputs()

    def _L0_gnn_setup():
        import jax, jax.numpy as jnp
        import numpy as np
        N = 50000
        E = 12500
        IN_DIM = 256
        H = 8
        D = 32
        LN_EPS = 1e-05
        key = jax.random.key(seed)
        k_x, k_e, k_w, k_a = jax.random.split(key, 4)
        x = jax.random.normal(k_x, (N, IN_DIM), dtype=jnp.float32)
        edge_index = jax.random.randint(k_e, (2, E), 0, N, dtype=jnp.int32)
        w_lim = np.sqrt(6.0 / (IN_DIM + H * D)) * np.sqrt(2.0)
        W = jax.random.uniform(k_w, (IN_DIM, H * D), minval=-w_lim, maxval=w_lim, dtype=jnp.float32)
        a_lim = np.sqrt(6.0 / (2 * D + 1))
        k_as, k_ad = jax.random.split(k_a)
        a_src = jnp.broadcast_to(jax.random.uniform(k_as, (1, D), minval=-a_lim, maxval=a_lim, dtype=jnp.float32), (H, D)).copy()
        a_dst = jnp.broadcast_to(jax.random.uniform(k_ad, (1, D), minval=-a_lim, maxval=a_lim, dtype=jnp.float32), (H, D)).copy()
        gamma = jnp.ones((H * D,), dtype=jnp.float32)
        beta = jnp.zeros((H * D,), dtype=jnp.float32)
        return {'x': x, 'edge_index': edge_index, 'W': W, 'a_src': a_src, 'a_dst': a_dst, 'gamma': gamma, 'beta': beta}
    _L0_gnn_all = _L0_gnn_setup()
    _L0_gnn_in = {k: v for k, v in _L0_gnn_all.items() if k in ('W', 'a_src', 'a_dst', 'gamma', 'beta')}
    del _L0_gnn_all

    def _L1_gnn_setup():
        import jax, jax.numpy as jnp
        import numpy as np
        N_NODES = 10000
        N_RAND_EDGES = 10000
        IN_DIM = 256
        HIDDEN = 64
        HEADS = 8
        OUT_DIM = 256
        NEG_SLOPE = 0.2

        def gat_conv(x, W, attn_l, attn_r, src, dst, n_nodes):
            H, D = attn_l.shape
            feat = (x @ W).reshape(n_nodes, H, D)
            el = jnp.einsum('nhd,hd->nh', feat, attn_l)
            er = jnp.einsum('nhd,hd->nh', feat, attn_r)
            e = jax.nn.leaky_relu(el[src] + er[dst], NEG_SLOPE)
            m = jax.ops.segment_max(e, dst, num_segments=n_nodes)
            ex = jnp.exp(e - m[dst])
            denom = jax.ops.segment_sum(ex, dst, num_segments=n_nodes)
            alpha = ex / denom[dst]
            out = jax.ops.segment_sum(alpha[:, :, None] * feat[src], dst, num_segments=n_nodes)
            return out.reshape(n_nodes, H * D)
        key = jax.random.key(seed)
        ks = jax.random.split(key, 9)
        h = jax.random.normal(ks[0], (N_NODES, IN_DIM), dtype=jnp.float32)
        src = jnp.concatenate([jax.random.randint(ks[1], (N_RAND_EDGES,), 0, N_NODES, dtype=jnp.int32), jnp.arange(N_NODES, dtype=jnp.int32)])
        dst = jnp.concatenate([jax.random.randint(ks[2], (N_RAND_EDGES,), 0, N_NODES, dtype=jnp.int32), jnp.arange(N_NODES, dtype=jnp.int32)])

        def glorot(k, shape):
            fan = shape[0] + shape[-1]
            s = jnp.sqrt(2.0 / fan).astype(jnp.float32)
            return jax.random.normal(k, shape, dtype=jnp.float32) * s
        W1 = glorot(ks[3], (IN_DIM, HEADS * HIDDEN))
        attn_l1 = glorot(ks[4], (HEADS, HIDDEN))
        attn_r1 = glorot(ks[5], (HEADS, HIDDEN))
        W2 = glorot(ks[6], (HEADS * HIDDEN, OUT_DIM))
        attn_l2 = glorot(ks[7], (1, OUT_DIM))
        attn_r2 = glorot(ks[8], (1, OUT_DIM))
        return {'h': h, 'W1': W1, 'attn_l1': attn_l1, 'attn_r1': attn_r1, 'W2': W2, 'attn_l2': attn_l2, 'attn_r2': attn_r2, 'src': src, 'dst': dst}
    _L1_gnn_all = _L1_gnn_setup()
    _L1_gnn_in = {k: v for k, v in _L1_gnn_all.items() if k in ('W1', 'attn_l1', 'attn_r1', 'W2', 'attn_l2', 'attn_r2')}
    del _L1_gnn_all

    def _L2_gnn_setup():
        import jax, jax.numpy as jnp
        import numpy as np
        N_NODES = 10000
        N_EDGES = 5000
        IN_FEATS = 256
        E_DIMS = 64
        NEG_SLOPE = 0.01
        key = jax.random.key(seed)
        ks = jax.random.split(key, 8)
        h = jax.random.normal(ks[0], (N_NODES, IN_FEATS), dtype=jnp.float32)
        w = jax.random.normal(ks[1], (N_EDGES, E_DIMS), dtype=jnp.float32)
        snorm_n = jax.random.uniform(ks[2], (N_NODES, 1), dtype=jnp.float32)
        edge_src = jax.random.randint(ks[3], (N_EDGES,), 0, N_NODES, dtype=jnp.int64)
        edge_dst = jax.random.randint(ks[4], (N_EDGES,), 0, N_NODES, dtype=jnp.int64)
        W_self = jax.random.normal(ks[5], (IN_FEATS, IN_FEATS), dtype=jnp.float32) * np.sqrt(2.0 / IN_FEATS)
        W_func = jax.random.normal(ks[6], (IN_FEATS, IN_FEATS), dtype=jnp.float32) * np.sqrt(2.0 / IN_FEATS)
        W_att = jax.random.normal(ks[7], (1, 2 * IN_FEATS + E_DIMS), dtype=jnp.float32) * np.sqrt(2.0 / (2 * IN_FEATS + E_DIMS))
        return {'h': h, 'w': w, 'snorm_n': snorm_n, 'edge_src': edge_src, 'edge_dst': edge_dst, 'W_self': W_self, 'W_func': W_func, 'W_att': W_att}
    _L2_gnn_all = _L2_gnn_setup()
    _L2_gnn_in = {k: v for k, v in _L2_gnn_all.items() if k in ('W_self', 'W_func', 'W_att')}
    del _L2_gnn_all

    def _L3_gnn_setup():
        import jax, jax.numpy as jnp
        import numpy as np
        N, IN_CH, HID, HEADS, OUT_CH, E = (30000, 256, 128, 4, 256, 15000)
        NEG_SLOPE = 0.2

        def gat_conv(x, W, a_src, a_dst, bias, src, dst, heads, out_ch, concat):
            n = x.shape[0]
            h = (x @ W).reshape(n, heads, out_ch)
            al_s = jnp.einsum('nhc,hc->nh', h, a_src)
            al_d = jnp.einsum('nhc,hc->nh', h, a_dst)
            logits = jax.nn.leaky_relu(al_s[src] + al_d[dst], NEG_SLOPE)
            m = jax.lax.stop_gradient(jax.ops.segment_max(logits, dst, num_segments=n))
            e = jnp.exp(logits - m[dst])
            denom = jax.ops.segment_sum(e, dst, num_segments=n)
            alpha = e / denom[dst]
            msg = h[src] * alpha[:, :, None]
            out = jax.ops.segment_sum(msg, dst, num_segments=n)
            out = out.reshape(n, heads * out_ch) if concat else out.mean(axis=1)
            return out + bias
        key = jax.random.key(seed)
        ks = jax.random.split(key, 12)
        s = lambda fin: 1.0 / np.sqrt(fin)
        return {'x': jax.random.normal(ks[0], (N, IN_CH), jnp.float32), 'edge_index': jax.random.randint(ks[1], (2, E), 0, N, jnp.int32), 'W1': jax.random.normal(ks[2], (IN_CH, HEADS * HID), jnp.float32) * s(IN_CH), 'a_src1': jax.random.normal(ks[3], (HEADS, HID), jnp.float32) * s(HID), 'a_dst1': jax.random.normal(ks[4], (HEADS, HID), jnp.float32) * s(HID), 'b1': jnp.zeros((HEADS * HID,), jnp.float32), 'prelu_w': jnp.asarray(0.25, jnp.float32), 'W2': jax.random.normal(ks[5], (HEADS * HID, OUT_CH), jnp.float32) * s(HEADS * HID), 'a_src2': jax.random.normal(ks[6], (1, OUT_CH), jnp.float32) * s(OUT_CH), 'a_dst2': jax.random.normal(ks[7], (1, OUT_CH), jnp.float32) * s(OUT_CH), 'b2': jnp.zeros((OUT_CH,), jnp.float32)}
    _L3_gnn_all = _L3_gnn_setup()
    _L3_gnn_in = {k: v for k, v in _L3_gnn_all.items() if k in ('W1', 'a_src1', 'a_dst1', 'b1', 'prelu_w', 'W2', 'a_src2', 'a_dst2', 'b2')}
    del _L3_gnn_all
    return {'x': x, 'src': src, 'dst': dst, 'edge_attr_64': edge_attr_64, 'node_vec1': node_vec1, 'L0_gnn_W': _L0_gnn_in['W'], 'L0_gnn_a_src': _L0_gnn_in['a_src'], 'L0_gnn_a_dst': _L0_gnn_in['a_dst'], 'L0_gnn_gamma': _L0_gnn_in['gamma'], 'L0_gnn_beta': _L0_gnn_in['beta'], 'L1_gnn_W1': _L1_gnn_in['W1'], 'L1_gnn_attn_l1': _L1_gnn_in['attn_l1'], 'L1_gnn_attn_r1': _L1_gnn_in['attn_r1'], 'L1_gnn_W2': _L1_gnn_in['W2'], 'L1_gnn_attn_l2': _L1_gnn_in['attn_l2'], 'L1_gnn_attn_r2': _L1_gnn_in['attn_r2'], 'L2_gnn_W_self': _L2_gnn_in['W_self'], 'L2_gnn_W_func': _L2_gnn_in['W_func'], 'L2_gnn_W_att': _L2_gnn_in['W_att'], 'L3_gnn_W1': _L3_gnn_in['W1'], 'L3_gnn_a_src1': _L3_gnn_in['a_src1'], 'L3_gnn_a_dst1': _L3_gnn_in['a_dst1'], 'L3_gnn_b1': _L3_gnn_in['b1'], 'L3_gnn_prelu_w': _L3_gnn_in['prelu_w'], 'L3_gnn_W2': _L3_gnn_in['W2'], 'L3_gnn_a_src2': _L3_gnn_in['a_src2'], 'L3_gnn_a_dst2': _L3_gnn_in['a_dst2'], 'L3_gnn_b2': _L3_gnn_in['b2']}

def reference(x, src, dst, edge_attr_64, node_vec1, L0_gnn_W, L0_gnn_a_src, L0_gnn_a_dst, L0_gnn_gamma, L0_gnn_beta, L1_gnn_W1, L1_gnn_attn_l1, L1_gnn_attn_r1, L1_gnn_W2, L1_gnn_attn_l2, L1_gnn_attn_r2, L2_gnn_W_self, L2_gnn_W_func, L2_gnn_W_att, L3_gnn_W1, L3_gnn_a_src1, L3_gnn_a_dst1, L3_gnn_b1, L3_gnn_prelu_w, L3_gnn_W2, L3_gnn_a_src2, L3_gnn_a_dst2, L3_gnn_b2):
    import jax
    import jax.numpy as jnp

    def _L0_gnn_ref(x, edge_index, W, a_src, a_dst, gamma, beta):
        import jax, jax.numpy as jnp
        import numpy as np
        N = 50000
        E = 12500
        IN_DIM = 256
        H = 8
        D = 32
        LN_EPS = 1e-05
        n = x.shape[0]
        src, dst = (edge_index[0], edge_index[1])
        hh = (x @ W).reshape(n, H, D)
        s_src = jnp.einsum('nhd,hd->nh', hh, a_src)
        s_dst = jnp.einsum('nhd,hd->nh', hh, a_dst)
        scores = jax.nn.leaky_relu(s_src[src] + s_dst[dst], negative_slope=0.2)
        m = jax.ops.segment_max(scores, dst, num_segments=n)
        e = jnp.exp(scores - m[dst])
        denom = jax.ops.segment_sum(e, dst, num_segments=n)
        alpha = e / denom[dst]
        msgs = hh[src] * alpha[:, :, None]
        out = jax.ops.segment_sum(msgs, dst, num_segments=n).reshape(n, H * D)
        out = out + x
        mu = jnp.mean(out, axis=-1, keepdims=True)
        var = jnp.mean(jnp.square(out - mu), axis=-1, keepdims=True)
        out = (out - mu) / jnp.sqrt(var + LN_EPS) * gamma + beta
        return jax.nn.elu(out)

    def _L1_gnn_ref(h, W1, attn_l1, attn_r1, W2, attn_l2, attn_r2, src, dst):
        import jax, jax.numpy as jnp
        import numpy as np
        N_NODES = 10000
        N_RAND_EDGES = 10000
        IN_DIM = 256
        HIDDEN = 64
        HEADS = 8
        OUT_DIM = 256
        NEG_SLOPE = 0.2

        def gat_conv(x, W, attn_l, attn_r, src, dst, n_nodes):
            H, D = attn_l.shape
            feat = (x @ W).reshape(n_nodes, H, D)
            el = jnp.einsum('nhd,hd->nh', feat, attn_l)
            er = jnp.einsum('nhd,hd->nh', feat, attn_r)
            e = jax.nn.leaky_relu(el[src] + er[dst], NEG_SLOPE)
            m = jax.ops.segment_max(e, dst, num_segments=n_nodes)
            ex = jnp.exp(e - m[dst])
            denom = jax.ops.segment_sum(ex, dst, num_segments=n_nodes)
            alpha = ex / denom[dst]
            out = jax.ops.segment_sum(alpha[:, :, None] * feat[src], dst, num_segments=n_nodes)
            return out.reshape(n_nodes, H * D)
        n = h.shape[0]
        x = gat_conv(h, W1, attn_l1, attn_r1, src, dst, n)
        x = jax.nn.elu(x)
        out = gat_conv(x, W2, attn_l2, attn_r2, src, dst, n)
        return out

    def _L2_gnn_ref(h, w, snorm_n, edge_src, edge_dst, W_self, W_func, W_att):
        import jax, jax.numpy as jnp
        import numpy as np
        N_NODES = 10000
        N_EDGES = 5000
        IN_FEATS = 256
        E_DIMS = 64
        NEG_SLOPE = 0.01
        N = h.shape[0]
        h_s = h @ W_self.T
        z = h @ W_func.T
        concat_z = jnp.concatenate([z[edge_src], z[edge_dst], w], axis=-1)
        e = jax.nn.leaky_relu(concat_z @ W_att.T, negative_slope=NEG_SLOPE)[:, 0]
        m = jax.ops.segment_max(e, edge_dst, num_segments=N)
        e_exp = jnp.exp(e - m[edge_dst])
        denom = jax.ops.segment_sum(e_exp, edge_dst, num_segments=N)
        alpha = e_exp / denom[edge_dst]
        agg = jax.ops.segment_sum(alpha[:, None] * z[edge_src], edge_dst, num_segments=N)
        h_new = h_s + agg
        deg = jax.ops.segment_sum(jnp.ones_like(e), edge_dst, num_segments=N)
        h_new = jnp.where(deg[:, None] > 0, h_new, h)
        h_new = jax.nn.relu(h_new)
        return h + h_new

    def _L3_gnn_ref(x, edge_index, W1, a_src1, a_dst1, b1, prelu_w, W2, a_src2, a_dst2, b2):
        import jax, jax.numpy as jnp
        import numpy as np
        N, IN_CH, HID, HEADS, OUT_CH, E = (30000, 256, 128, 4, 256, 15000)
        NEG_SLOPE = 0.2

        def gat_conv(x, W, a_src, a_dst, bias, src, dst, heads, out_ch, concat):
            n = x.shape[0]
            h = (x @ W).reshape(n, heads, out_ch)
            al_s = jnp.einsum('nhc,hc->nh', h, a_src)
            al_d = jnp.einsum('nhc,hc->nh', h, a_dst)
            logits = jax.nn.leaky_relu(al_s[src] + al_d[dst], NEG_SLOPE)
            m = jax.lax.stop_gradient(jax.ops.segment_max(logits, dst, num_segments=n))
            e = jnp.exp(logits - m[dst])
            denom = jax.ops.segment_sum(e, dst, num_segments=n)
            alpha = e / denom[dst]
            msg = h[src] * alpha[:, :, None]
            out = jax.ops.segment_sum(msg, dst, num_segments=n)
            out = out.reshape(n, heads * out_ch) if concat else out.mean(axis=1)
            return out + bias
        n = x.shape[0]
        loop = jnp.arange(n, dtype=edge_index.dtype)
        src = jnp.concatenate([edge_index[0], loop])
        dst = jnp.concatenate([edge_index[1], loop])
        h = gat_conv(x, W1, a_src1, a_dst1, b1, src, dst, HEADS, HID, concat=True)
        h = jnp.where(h >= 0, h, prelu_w * h)
        z = gat_conv(h, W2, a_src2, a_dst2, b2, src, dst, 1, OUT_CH, concat=False)
        return z
    edge_index = jnp.stack([src, dst])
    h = jnp.maximum(_layernorm(x, axis=-1), 0.0)
    x = x + _L0_gnn_ref(h, edge_index, L0_gnn_W, L0_gnn_a_src, L0_gnn_a_dst, L0_gnn_gamma, L0_gnn_beta)
    h = jnp.maximum(_layernorm(x, axis=-1), 0.0)
    x = x + _L1_gnn_ref(h, L1_gnn_W1, L1_gnn_attn_l1, L1_gnn_attn_r1, L1_gnn_W2, L1_gnn_attn_l2, L1_gnn_attn_r2, src, dst)
    h = jnp.maximum(_layernorm(x, axis=-1), 0.0)
    x = x + _L2_gnn_ref(h, edge_attr_64, node_vec1, src, dst, L2_gnn_W_self, L2_gnn_W_func, L2_gnn_W_att)
    h = jnp.maximum(_layernorm(x, axis=-1), 0.0)
    x = x + _L3_gnn_ref(h, edge_index, L3_gnn_W1, L3_gnn_a_src1, L3_gnn_a_dst1, L3_gnn_b1, L3_gnn_prelu_w, L3_gnn_W2, L3_gnn_a_src2, L3_gnn_a_dst2, L3_gnn_b2)
    return x

_drawn_inputs = setup_inputs


def setup_inputs(seed=0):
    import zlib

    import numpy as np

    out = dict(_drawn_inputs(seed))
    spreads = {'L0_gnn_gamma': (1.0, 0.2),
     'L0_gnn_beta': (0.0, 0.1),
     'L3_gnn_b1': (0.0, 0.339),
     'L3_gnn_b2': (0.0, 0.1)}
    factors = {'L1_gnn_attn_l1': 3.097,
     'L1_gnn_attn_r1': 8.0,
     'L1_gnn_attn_l2': 8.0,
     'L1_gnn_attn_r2': 8.0,
     'L3_gnn_a_src1': 6.478,
     'L3_gnn_a_dst1': 8.0,
     'L3_gnn_a_src2': 8.0,
     'L3_gnn_a_dst2': 45.767}
    for name, (base, spread) in spreads.items():
        noise = np.random.default_rng([zlib.crc32(name.encode()), seed]).standard_normal(out[name].shape)
        drawn = base * np.exp(spread * noise) if base else spread * noise
        out[name] = jnp.asarray(drawn.astype(out[name].dtype))
    for name, factor in factors.items():
        out[name] = (out[name] * factor).astype(out[name].dtype)
    return out
```

```python
from contextlib import ExitStack

import concourse.bass as bass
import concourse.mybir as mybir

F32 = mybir.dt.float32
BF16 = mybir.dt.bfloat16
I32 = mybir.dt.int32
ALU = mybir.AluOpType
ACT = mybir.ActivationFunctionType
AX_X = mybir.AxisListType.X

P = 128
NODES = 3125
EDGES = 50000
DIM = 256
EDGE_DIM = 64
BLOCKS = -(-NODES // P)
TILES = -(-EDGES // P)
GROUP = 8
GROUPS = -(-(TILES + BLOCKS - 1) // GROUP)
STEPS = GROUPS * GROUP
STEP_ROWS = -(-STEPS // P)
NO_NODE = 4095
LN_EPS = 1e-5
LOW = -1e30
TINY = 1e-30
MAX_HEADS = 8
MAX_ACC = 528


class Stage:

    def __init__(self, nc, ctx, name):
        self.sem = ctx.enter_context(nc.semaphore(name))
        self.base = 0

    def wait(self, eng, count):
        if isinstance(count, int) and count <= 0:
            return
        eng.wait_ge(self.sem, self.base + count)


class Layer:

    def __init__(self, heads, depth, k, slope, self_loop=False, edge_term=False, extra=0):
        self.heads, self.depth, self.k, self.slope = heads, depth, k, slope
        self.self_loop, self.edge_term, self.extra = self_loop, edge_term, extra
        self.feat = heads * depth
        self.row = self.feat + heads
        self.acc = self.feat + (2 if self_loop else 1) * heads
        self.proj = self.feat + 2 * heads + extra
        self.chunks = k // P


LAYERS = [
    Layer(8, 32, 256, 0.2),
    Layer(8, 64, 256, 0.2),
    Layer(1, 256, 512, 0.2),
    Layer(1, 256, 256, 0.01, edge_term=True, extra=256),
    Layer(4, 128, 256, 0.2, self_loop=True),
    Layer(1, 256, 512, 0.2, self_loop=True),
]


def per_head(ap, heads):
    return ap.rearrange("p (h d) -> p h d", h=heads)


def prepare(nc, ctx, st, io, sb):
    row_of = io["walk_rows"]
    with ExitStack() as c:
        def tmp(name, shape, dt=F32):
            return c.enter_context(nc.sbuf_tensor(name, shape, dt))

        def sem(name):
            return c.enter_context(nc.semaphore(name))

        last = tmp("last_dst", [P, TILES - 1], I32)
        leave = tmp("leave_step", [P, TILES - 1])
        iota_tiles = tmp("iota_tiles", [P, TILES - 1])
        passed = tmp("passed", [P, TILES - 1])
        step_no = tmp("step_no", [P, STEP_ROWS])
        tile_f = tmp("tile_f", [P, STEP_ROWS])
        tile_i = tmp("tile_i", [P, STEP_ROWS], I32)
        block_f = tmp("block_f", [P, STEP_ROWS])
        block_i = tmp("block_i", [P, STEP_ROWS], I32)
        src_rows = tmp("src_rows", [P, STEP_ROWS, P], I32)
        dst_rows = tmp("dst_rows", [P, STEP_ROWS, P], I32)
        dst_before = tmp("dst_before", [P, STEP_ROWS, P], I32)
        dst_after = tmp("dst_after", [P, STEP_ROWS, P], I32)
        ea_rows = tmp("ea_rows", [P, STEP_ROWS, P])
        src_f = tmp("src_f", [P, STEP_ROWS, P])
        dst_f = tmp("dst_f", [P, STEP_ROWS, P])
        starts = tmp("starts", [P, STEP_ROWS, P])
        ends = tmp("ends", [P, STEP_ROWS, P])
        pen = tmp("pen", [P, 2, STEP_ROWS, P], BF16)
        att_e = tmp("att_e", [P, EDGE_DIM])
        EPP = TILES
        NCH = 4
        CH = -(-EPP // NCH)
        ea_in = tmp("ea_in", [P, 2, CH * EDGE_DIM])
        ea_out = tmp("ea_out", [P, TILES])
        psum = [c.enter_context(nc.psum_tensor(f"turn{k}", [P, 512], F32)) for k in range(5)]

        s_in, s_att, s_t, s_b, s_ea_st, s_seq, s_sh, s_bi = (sem(n) for n in (
            "prep_in", "att_in", "tile_index", "block_store", "ea_store", "walk_dst_store", "shifted", "block_row"))
        s_eain = [sem("ea_in0"), sem("ea_in1")]
        s_g = [sem("src_got"), sem("dst_got"), sem("ea_got")]
        s_eadone, s_walk, s_mark, s_pen, s_turned, s_dve = (sem(n) for n in (
            "ea_chunk_done", "walk_f_ready", "marks_ready", "pen_store", "tables_turned", "prep_done"))
        blk = c.enter_context(nc.Block())

        @blk.sync
        def _(sp):
            sp.dma_start(last[:, :], io["dst_last"].partition_broadcast(P)).then_inc(s_in, 16)
            sp.dma_start(iota_tiles[:, :], io["iota"][0:TILES - 1].partition_broadcast(P)).then_inc(s_in, 16)
            sp.dma_start(step_no[:, :], io["step_no"][:, :]).then_inc(s_in, 16)
            sp.dma_start(sb["ident"][:, :], io["ident"][:, :]).then_inc(s_in, 16)
            sp.dma_start(sb["iota"][:, :], io["iota"][0:P].partition_broadcast(P)).then_inc(s_in, 16)
            sp.dma_start(att_e[:, :], io["att"][2 * DIM:2 * DIM + EDGE_DIM].partition_broadcast(P)).then_inc(s_att, 16)
            for n in range(NCH):
                w = min(CH, EPP - n * CH)
                if n >= 2:
                    sp.wait_ge(s_eadone, n - 1)
                sp.dma_start(ea_in[:, n % 2, 0:w * EDGE_DIM],
                             io["edge_attr"][:, n * CH * EDGE_DIM:(n * CH + w) * EDGE_DIM]).then_inc(s_eain[n % 2], 16)
            sp.wait_ge(s_eadone, NCH)
            sp.dma_start(io["ea_flat"][:, :], ea_out[:, :]).then_inc(s_ea_st, 16)
            sp.wait_ge(s_t, 2)
            with nc.allow_non_contiguous_dma(reason="one number per step"):
                sp.dma_start(io["walk_block"].rearrange("(k p) -> p k", p=P), block_i[:, :]).then_inc(s_b, 16)
            sp.wait_ge(s_b, 16)
            sp.dma_start(sb["block_of"][0:1, :], io["walk_block"][0:STEPS].unsqueeze(0)).then_inc(s_bi, 16)
            sp.wait_ge(s_g[1], 16 * STEP_ROWS)
            seq = row_of[P:P + STEP_ROWS * P * P].rearrange("(k p q) -> p k q", p=P, q=P)
            sp.dma_start(seq, dst_rows[:, :, :]).then_inc(s_seq, 16)
            sp.dma_start(row_of[0:P].unsqueeze(0), io["no_node"].unsqueeze(0)).then_inc(s_seq, 16)
            sp.dma_start(row_of[P + STEP_ROWS * P * P:2 * P + STEP_ROWS * P * P].unsqueeze(0),
                         io["no_node"].unsqueeze(0)).then_inc(s_seq, 16)
            sp.wait_ge(s_seq, 48)
            for buf, off in ((dst_before, P - 1), (dst_after, P + 1)):
                view = row_of[off:off + STEP_ROWS * P * P].rearrange("(k p q) -> p k q", p=P, q=P)
                sp.dma_start(buf[:, :, :], view).then_inc(s_sh, 16)
            sp.wait_ge(s_mark, 1)
            for d in range(2):
                view = io["pen"][d].rearrange("(k p q) -> p k q", p=P, q=P)
                sp.dma_start(view, pen[:, d, :, :]).then_inc(s_pen, 16)
            sp.wait_ge(s_pen, 32)
            sp.wait_ge(s_bi, 16)

        @blk.gpsimd
        def _(pool):
            pool.wait_ge(s_t, 1)
            for k in range(STEP_ROWS):
                for buf, table, s in ((src_rows, "src_tiles", s_g[0]), (dst_rows, "dst_tiles", s_g[1])):
                    nc.gpsimd.indirect_dma_start(
                        out=buf[:, k, :], out_offset=None, in_=io[table][:, :],
                        in_offset=bass.IndirectOffsetOnAxis(ap=tile_i[:, k:k + 1], axis=0)).then_inc(s, 16)
            pool.wait_ge(s_ea_st, 16)
            for k in range(STEP_ROWS):
                nc.gpsimd.indirect_dma_start(
                    out=ea_rows[:, k, :], out_offset=None, in_=io["ea_tiles"][:, :],
                    in_offset=bass.IndirectOffsetOnAxis(ap=tile_i[:, k:k + 1], axis=0)).then_inc(s_g[2], 16)

        @blk.vector
        def _(dve):
            v = nc.vector
            dve.wait_ge(s_in, 80)
            v.tensor_scalar(last[:, :], last[:, :], 7, None, ALU.arith_shift_right)
            v.drain()
            v.tensor_tensor(leave[:, :], last[:, :], iota_tiles[:, :], ALU.add)
            v.drain()
            for k in range(STEP_ROWS):
                v.tensor_scalar(passed[:, :], leave[:, :], step_no[:, k:k + 1], None, ALU.is_lt)
                v.drain()
                v.tensor_reduce(tile_f[:, k:k + 1], passed[:, :], AX_X, ALU.add)
                v.drain()
            v.tensor_copy(tile_i[:, :], tile_f[:, :]).then_inc(s_t, 1)
            v.tensor_tensor(block_f[:, :], step_no[:, :], tile_f[:, :], ALU.subtract)
            v.drain()
            v.tensor_scalar(block_i[:, :], block_f[:, :], float(BLOCKS - 1), None, ALU.min).then_inc(s_t, 1)
            v.tensor_scalar(block_f[:, :], block_f[:, :], float(P), None, ALU.mult)
            dve.wait_ge(s_att, 16)
            for n in range(NCH):
                w = min(CH, EPP - n * CH)
                dve.wait_ge(s_eain[n % 2], 16 * (n // 2 + 1))
                view = ea_in[:, n % 2, 0:w * EDGE_DIM].rearrange("p (j d) -> p j d", d=EDGE_DIM)
                v.tensor_tensor(view, view, att_e[:, :].unsqueeze(1).to_broadcast([P, w, EDGE_DIM]), ALU.mult)
                v.drain()
                v.tensor_reduce(ea_out[:, n * CH:n * CH + w], view, AX_X, ALU.add).then_inc(s_eadone, 1)
            dve.wait_ge(s_g[0], 16 * STEP_ROWS)
            dve.wait_ge(s_g[1], 16 * STEP_ROWS)
            v.tensor_copy(src_f[:, :, :], src_rows[:, :, :])
            for k in range(STEP_ROWS):
                v.tensor_scalar(dst_f[:, k, :], dst_rows[:, k, :], block_f[:, k:k + 1], None, ALU.subtract)
            v.drain().then_inc(s_walk, 1)
            dve.wait_ge(s_sh, 32)
            v.tensor_tensor(starts[:, :, :], dst_rows[:, :, :], dst_before[:, :, :], ALU.not_equal)
            v.tensor_tensor(ends[:, :, :], dst_rows[:, :, :], dst_after[:, :, :], ALU.not_equal)
            v.drain()
            v.tensor_scalar(pen[:, 0, :, :], starts[:, :, :], LOW, None, ALU.mult)
            v.tensor_scalar(pen[:, 1, :, :], ends[:, :, :], LOW, None, ALU.mult)
            v.drain().then_inc(s_mark, 1)
            for n, (dst, dt) in enumerate(((sb["src_of"], I32), (sb["dst_in_block"], F32), (sb["ends_here"], F32),
                                           (passed, F32), (sb["edge_term"], F32))):
                dve.wait_ge(s_turned, n + 1)
                if n == 3:
                    v.tensor_copy(src_f[:, 0, 0:GROUPS], psum[n][:, 0:STEPS:GROUP])
                else:
                    v.tensor_copy(dst[:, :], psum[n][:, 0:STEPS])
            v.drain()
            v.tensor_scalar(src_f[:, 0, 0:GROUPS], src_f[:, 0, 0:GROUPS], -1.0, 1.0, ALU.mult, ALU.add)
            v.drain()
            v.tensor_scalar(sb["goes_on"][:, :], src_f[:, 0, 0:GROUPS], sb["ident"][:, 0:1], None, ALU.mult)
            v.drain().then_inc(s_dve, 1)

        @blk.tensor
        def _(pe):
            pe.wait_ge(s_in, 80)
            for n, rows in enumerate((src_f, dst_f, ends, starts, ea_rows)):
                if n == 0:
                    pe.wait_ge(s_walk, 1)
                if n == 2:
                    pe.wait_ge(s_mark, 1)
                if n == 4:
                    pe.wait_ge(s_g[2], 16 * STEP_ROWS)
                for k in range(STEP_ROWS):
                    mm = nc.tensor.transpose(psum[n][:, k * P:(k + 1) * P], rows[:, k, :], sb["ident"][:, :])
                mm.then_inc(s_turned, 1)


def node_phase(nc, st, io, sb, n):
    L = LAYERS[n] if n < len(LAYERS) else None
    prev = LAYERS[n - 1] if n else None
    loads = {0: ["x"], 1: ["h"], 2: [], 3: ["x"], 4: ["x", "h", "hs"], 5: ["table"], 6: ["x", "table"]}[n]
    if n == 1:
        loads = ["x", "h"]
    stores = {0: ["h"], 1: ["x"], 2: [], 3: ["x", "h"], 4: ["x"], 5: [], 6: ["out"]}[n]
    with ExitStack() as c:
        def tmp(name, shape, dt=F32):
            return c.enter_context(nc.sbuf_tensor(f"n{n}_{name}", shape, dt))

        width = {"x": DIM, "h": DIM, "hs": DIM, "table": prev.row if prev else 0}
        tin = {name: tmp("in_" + name, [P, 2, width[name]]) for name in loads}
        xo = tmp("x_out", [P, 2, DIM])
        k_in = L.k if L else DIM
        h = tmp("h", [P, 2, 512])
        a = tmp("a", [P, 512])
        b = tmp("b", [P, 512])
        e = tmp("e", [P, 512])
        small = tmp("small", [P, 96])
        vec = tmp("vec", [P, 2, 512])
        vec1 = tmp("vec1", [P, 1])
        psum_t = [c.enter_context(nc.psum_tensor(f"n{n}_ps_hT{p}", [P, 512], F32)) for p in range(2)]
        psum_f = [c.enter_context(nc.psum_tensor(f"n{n}_ps_proj{p}", [P, 1024], F32)) for p in range(2)]
        if L:
            wx = tmp("wx", [P, L.chunks, L.proj])
            wtmp = tmp("wtmp", [P, 512])
            avec = tmp("avec", [P, 2, L.feat])
            hT = tmp("hT", [P, 2, 512])
            tb = tmp("tb", [P, 2, L.row + L.extra])
        split = min(512, L.proj) if L else 0
        if L and L.extra:
            split = L.feat + 2 * L.heads
        blk = c.enter_context(nc.Block())

        dram = {"x": io["x"] if n <= 1 else io["x_mid"], "h": io["h_mid"], "hs": io["hs_mid"],
                "table": io[f"rows{n - 1}"] if n else None}
        sto = {"x": io["x_mid"], "h": io["h_mid"], "out": io["out"]}

        def rows(t):
            return bass.ds(t * P, P)

        def slots(fn, eng):
            fn(0, 0)
            fn(1, 1)
            with eng.Fori(0, (BLOCKS - 3) // 2) as i:
                for p in range(2):
                    fn(2 * i + 2 + p, p)
            for t in range(BLOCKS - 1, BLOCKS + 1):
                fn(t, t % 2)

        @blk.sync
        def _(sp):
            nw = 0
            if L:
                wsrc = io[f"w{n}"]
                for k in range(L.chunks):
                    sp.dma_start(wx[:, k, 0:L.feat], wsrc[k * P:(k + 1) * P, 0:L.feat]).then_inc(st["w_in"].sem, 16)
                    if L.extra:
                        sp.dma_start(wx[:, k, L.feat + 2 * L.heads:], wsrc[k * P:(k + 1) * P, L.feat:]).then_inc(
                            st["w_in"].sem, 16)
                    nw += 2 if L.extra else 1
                for j in range(2):
                    sp.dma_start(avec[:, j, :], io[f"a{n}"][j].partition_broadcast(P)).then_inc(st["w_in"].sem, 16)
                    nw += 1
            if n == 1:
                sp.dma_start(vec[:, 0, 0:DIM], io["gamma"].partition_broadcast(P)).then_inc(st["w_in"].sem, 16)
                sp.dma_start(vec[:, 1, 0:DIM], io["beta"].partition_broadcast(P)).then_inc(st["w_in"].sem, 16)
                nw += 2
            if n == 5:
                sp.dma_start(vec[:, 0, :], io["b1"].partition_broadcast(P)).then_inc(st["w_in"].sem, 16)
                sp.dma_start(vec1[:, :], io["prelu"].partition_broadcast(P)).then_inc(st["w_in"].sem, 16)
                nw += 2
            if n == 6:
                sp.dma_start(vec[:, 0, 0:DIM], io["b2"].partition_broadcast(P)).then_inc(st["w_in"].sem, 16)
                nw += 1
            sb["n_w"] = nw

            def load(t, p):
                st["pre_done"].wait(sp, t - 1)
                for name in loads:
                    sp.dma_start(tin[name][:, p, :], dram[name][rows(t), 0:width[name]]).then_inc(
                        st[f"in{p}"].sem, 16)

            def slot(t, p):
                if not (isinstance(t, int) and t >= BLOCKS) and loads:
                    load(t, p)
                if not (isinstance(t, int) and t == 0):
                    u, q = t - 1, 1 - p
                    if stores:
                        st["pre_done"].wait(sp, u + 1)
                    for name in stores:
                        src = {"x": xo, "out": xo, "h": h}[name]
                        sp.dma_start(sto[name][rows(u), 0:DIM], src[:, q, 0:DIM]).then_inc(st[f"out{q}"].sem, 16)
                    if L:
                        st["table_sb"].wait(sp, u + 1)
                        sp.dma_start(io[f"rows{n}"][rows(u), 0:L.row], tb[:, q, 0:L.row]).then_inc(st[f"tb{q}"].sem, 16)
                        if L.extra:
                            sp.dma_start(io["hs_mid"][rows(u), :], tb[:, q, L.row:]).then_inc(st[f"tb{q}"].sem, 16)

            slots(slot, sp)
            for p in range(2):
                tiles = (BLOCKS + 1 - p) // 2
                if stores:
                    st[f"out{p}"].wait(sp, 16 * tiles * len(stores))
                if L:
                    st[f"tb{p}"].wait(sp, 16 * tiles * (2 if L.extra else 1))

        @blk.vector
        def _(dve):
            v = nc.vector
            st["w_in"].wait(dve, 16 * sb["n_w"])
            if L:
                for k in range(L.chunks):
                    for j in range(2):
                        v.tensor_tensor(wtmp[:, 0:L.feat], wx[:, k, 0:L.feat], avec[:, j, :], ALU.mult)
                        v.drain()
                        v.tensor_reduce(wx[:, k, L.feat + j * L.heads:L.feat + (j + 1) * L.heads],
                                        per_head(wtmp[:, 0:L.feat], L.heads), AX_X, ALU.add)
                        v.drain()
                v.drain().then_inc(st["w_ready"].sem, 1)

            def norm(dst, src, count, relu=True):
                v.bn_stats(small[:, 0:6], src)
                v.drain()
                v.bn_aggr(small[:, 6:8], small[:, 0:6])
                v.drain()
                v.tensor_scalar(small[:, 8:9], small[:, 7:8], LN_EPS, None, ALU.add)
                v.tensor_scalar(dst, src, small[:, 6:7], 0.0 if relu else None, ALU.subtract,
                                ALU.max if relu else ALU.bypass)
                v.drain().then_inc(st["variance"].sem, 1)
                st["inv_std"].wait(dve, count)
                v.tensor_scalar(dst, dst, small[:, 9:10], None, ALU.mult)
                v.drain()

            def exp_of(t, width_):
                v.tensor_scalar(e[:, 0:width_], a[:, 0:width_], 0.0, None, ALU.min)
                v.drain().then_inc(st["exp_in"].sem, 1)
                st["exp_out"].wait(dve, t + 1)

            def sums(t):
                return sb["acc"][:, bass.ds(t * prev.acc, prev.acc)]

            def divide(dst, t):
                A = sums(t)
                H, F = prev.heads, prev.feat
                v.tensor_scalar(small[:, 16:16 + H], A[:, F:F + H], TINY, None, ALU.max)
                v.drain()
                v.reciprocal(small[:, 24:24 + H], small[:, 16:16 + H])
                v.drain()
                v.tensor_tensor(per_head(dst, H), per_head(A[:, 0:F], H),
                                small[:, 24:24 + H].unsqueeze(2).to_broadcast([P, H, prev.depth]), ALU.mult)
                v.drain()

            def join_self(t, p):
                A = sums(t)
                H, F, D = prev.heads, prev.feat, prev.depth
                own = tin["table"]
                er = sb["er"][:, bass.ds(t * H, H)]
                den, top = A[:, F:F + H], A[:, F + H:F + 2 * H]
                s = lambda i, m=1: small[:, 16 + 8 * i:16 + 8 * i + m * H]
                v.tensor_scalar(s(0), den, 0.5, None, ALU.is_lt)
                v.drain()
                v.scalar_tensor_tensor(s(1), s(0), LOW, top, ALU.mult, ALU.add)
                v.drain()
                v.tensor_tensor(s(2), s(1), own[:, p, F:F + H], ALU.max)
                v.drain()
                v.tensor_tensor(s(1), s(1), er, ALU.add)
                v.tensor_tensor(s(2), s(2), er, ALU.add)
                v.tensor_tensor(s(3), own[:, p, F:F + H], er, ALU.add)
                v.drain()
                for i in (1, 2, 3):
                    v.scalar_tensor_tensor(s(i), s(i), prev.slope, s(i), ALU.mult, ALU.max)
                v.drain()
                v.tensor_tensor(e[:, 0:H], s(1), s(2), ALU.subtract)
                v.tensor_tensor(e[:, H:2 * H], s(3), s(2), ALU.subtract)
                v.drain().then_inc(st["exp_in"].sem, 1)
                st["exp_out"].wait(dve, t + 1)
                v.tensor_tensor(s(4), den, e[:, 0:H], ALU.mult)
                v.tensor_tensor(per_head(a[:, 0:F], H), per_head(A[:, 0:F], H),
                                e[:, 0:H].unsqueeze(2).to_broadcast([P, H, D]), ALU.mult)
                v.tensor_tensor(per_head(b[:, 0:F], H), per_head(own[:, p, 0:F], H),
                                e[:, H:2 * H].unsqueeze(2).to_broadcast([P, H, D]), ALU.mult)
                v.drain()
                v.tensor_tensor(s(4), s(4), e[:, H:2 * H], ALU.add)
                v.tensor_tensor(a[:, 0:F], a[:, 0:F], b[:, 0:F], ALU.add)
                v.drain()
                v.reciprocal(s(5), s(4))
                v.drain()
                v.tensor_tensor(per_head(a[:, 0:F], H), per_head(a[:, 0:F], H),
                                s(5).unsqueeze(2).to_broadcast([P, H, D]), ALU.mult)
                v.drain()

            def slot(t, p):
                if isinstance(t, int) and t >= BLOCKS:
                    return
                if L:
                    st["hT_ps"].wait(dve, t - 1)
                if stores:
                    if isinstance(t, int):
                        st[f"out{p}"].wait(dve, 16 * len(stores) * (t // 2))
                    else:
                        st[f"out{p}"].wait(dve, 8 * len(stores) * (t - p))
                if loads:
                    if isinstance(t, int):
                        st[f"in{p}"].wait(dve, 16 * len(loads) * (t // 2 + 1))
                    else:
                        st[f"in{p}"].wait(dve, 8 * len(loads) * (t - p) + 16 * len(loads))
                x_in = tin["x"][:, p, :] if "x" in tin else None
                xn, hn = xo[:, p, :], h[:, p, 0:DIM]
                if n == 0:
                    norm(hn, x_in, t + 1)
                elif n == 1:
                    divide(a[:, 0:DIM], t)
                    v.tensor_tensor(a[:, 0:DIM], a[:, 0:DIM], tin["h"][:, p, :], ALU.add)
                    v.drain()
                    norm(b[:, 0:DIM], a[:, 0:DIM], 2 * t + 1, relu=False)
                    v.tensor_tensor(b[:, 0:DIM], b[:, 0:DIM], vec[:, 0, 0:DIM], ALU.mult)
                    v.drain()
                    v.tensor_tensor(a[:, 0:DIM], b[:, 0:DIM], vec[:, 1, 0:DIM], ALU.add)
                    v.drain()
                    exp_of(t, DIM)
                    v.scalar_tensor_tensor(b[:, 0:DIM], e[:, 0:DIM], -1.0, x_in, ALU.add, ALU.add)
                    v.drain()
                    v.scalar_tensor_tensor(xn, a[:, 0:DIM], 0.0, b[:, 0:DIM], ALU.max, ALU.add)
                    v.drain()
                    norm(hn, xn, 2 * t + 2)
                elif n == 2:
                    divide(a[:, :], t)
                    exp_of(t, 512)
                    v.tensor_scalar(b[:, :], e[:, :], -1.0, None, ALU.add)
                    v.drain()
                    v.scalar_tensor_tensor(h[:, p, :], a[:, :], 0.0, b[:, :], ALU.max, ALU.add)
                    v.drain()
                elif n == 3:
                    divide(a[:, 0:DIM], t)
                    v.tensor_tensor(xn, a[:, 0:DIM], x_in, ALU.add)
                    v.drain()
                    norm(hn, xn, t + 1)
                elif n == 4:
                    divide(a[:, 0:DIM], t)
                    hp = tin["h"][:, p, :]
                    v.tensor_tensor(a[:, 0:DIM], a[:, 0:DIM], tin["hs"][:, p, :], ALU.add)
                    v.tensor_scalar(small[:, 32:33], sums(t)[:, DIM:DIM + 1], 0.5, None, ALU.is_gt)
                    v.tensor_scalar(small[:, 33:34], sums(t)[:, DIM:DIM + 1], 0.5, None, ALU.is_lt)
                    v.drain()
                    v.tensor_scalar(a[:, 0:DIM], a[:, 0:DIM], small[:, 32:33], None, ALU.mult)
                    v.drain()
                    v.scalar_tensor_tensor(a[:, 0:DIM], hp, small[:, 33:34], a[:, 0:DIM], ALU.mult, ALU.add)
                    v.drain()
                    v.scalar_tensor_tensor(b[:, 0:DIM], a[:, 0:DIM], 0.0, hp, ALU.max, ALU.add)
                    v.drain()
                    v.tensor_tensor(xn, b[:, 0:DIM], x_in, ALU.add)
                    v.drain()
                    norm(hn, xn, t + 1)
                elif n == 5:
                    join_self(t, p)
                    v.tensor_tensor(a[:, :], a[:, :], vec[:, 0, :], ALU.add)
                    v.drain()
                    v.tensor_scalar(b[:, :], a[:, :], 0.0, vec1[:, 0:1], ALU.min, ALU.mult)
                    v.drain()
                    v.scalar_tensor_tensor(h[:, p, :], a[:, :], 0.0, b[:, :], ALU.max, ALU.add)
                    v.drain()
                elif n == 6:
                    join_self(t, p)
                    v.tensor_tensor(a[:, 0:DIM], a[:, 0:DIM], vec[:, 0, 0:DIM], ALU.add)
                    v.drain()
                    v.tensor_tensor(xn, a[:, 0:DIM], x_in, ALU.add)
                v.drain().then_inc(st["pre_done"].sem, 1)

            slots(slot, dve)
            if L:
                for b0 in range(0, BLOCKS * L.acc, 4096):
                    v.memset(sb["acc"][:, b0:min(b0 + 4096, BLOCKS * L.acc)], 0.0)
                v.memset(sb["carry"][:, :], 0.0)

        norms = {0: 1, 1: 2, 3: 1, 4: 1}.get(n, 0)
        if norms:
            @blk.gpsimd
            def _(pool):
                def slot(t, p):
                    if isinstance(t, int) and t >= BLOCKS:
                        return
                    for j in range(norms):
                        st["variance"].wait(pool, norms * t + j + 1)
                        nc.gpsimd.tensor_tensor(small[:, 9:10], small[:, 8:9], sb["minus_half"][:, :],
                                                ALU.pow).then_inc(st["inv_std"].sem, 1)

                slots(slot, pool)

        @blk.scalar
        def _(act):
            uses_exp = n in (1, 2, 5, 6)
            ew = {1: DIM, 2: 512, 5: 2 * prev.heads, 6: 2 * prev.heads}[n] if uses_exp else 0

            def slot(t, p):
                final = isinstance(t, int) and t >= BLOCKS
                if not final:
                    if uses_exp:
                        st["exp_in"].wait(act, t + 1)
                        nc.scalar.activation(e[:, 0:ew], e[:, 0:ew], ACT.Exp).then_inc(st["exp_out"].sem, 1)
                    if L:
                        st["proj_ps"].wait(act, t - 1)
                        st["hT_ps"].wait(act, t + 1)
                        nc.scalar.activation(hT[:, p, 0:L.k], psum_t[p][:, 0:L.k], ACT.Copy).then_inc(
                            st["hT_sb"].sem, 1)
                if L and not (isinstance(t, int) and t == 0):
                    u, q = t - 1, 1 - p
                    k = 16 * (2 if L.extra else 1)
                    if isinstance(u, int):
                        st[f"tb{q}"].wait(act, k * (u // 2))
                    else:
                        st[f"tb{q}"].wait(act, (k // 2) * (u - q))
                    st["proj_ps"].wait(act, u + 1)
                    F, H = L.feat, L.heads
                    nc.scalar.activation(tb[:, q, 0:L.row], psum_f[q][:, 0:L.row], ACT.Copy)
                    if L.extra:
                        nc.scalar.activation(tb[:, q, L.row:], psum_f[q][:, 512:512 + L.extra], ACT.Copy)
                    nc.scalar.activation(sb["er"][:, bass.ds(u * H, H)], psum_f[q][:, F + H:F + 2 * H],
                                         ACT.Copy).then_inc(st["table_sb"].sem, 1)

            if L or uses_exp:
                slots(slot, act)

        if L:
            @blk.tensor
            def _(pe):
                st["w_ready"].wait(pe, 1)

                def slot(t, p):
                    if not (isinstance(t, int) and t >= BLOCKS):
                        st["hT_sb"].wait(pe, t - 1)
                        st["pre_done"].wait(pe, t + 1)
                        for k in range(L.chunks):
                            mm = nc.tensor.transpose(psum_t[p][:, k * P:(k + 1) * P], h[:, p, k * P:(k + 1) * P],
                                                     sb["ident"][:, :])
                        mm.then_inc(st["hT_ps"].sem, 1)
                    if not (isinstance(t, int) and t == 0):
                        u, q = t - 1, 1 - p
                        st["table_sb"].wait(pe, u - 1)
                        st["hT_sb"].wait(pe, u + 1)
                        for lo, hi, at in ((0, split, 0), (split, L.proj, 512)):
                            for k in range(L.chunks):
                                if lo < hi:
                                    mm = nc.tensor.matmul(psum_f[q][:, at:at + hi - lo], hT[:, q, k * P:(k + 1) * P],
                                                          wx[:, k, lo:hi], start=(k == 0), stop=(k == L.chunks - 1))
                        mm.then_inc(st["proj_ps"].sem, 1)

                slots(slot, pe)

    even = (BLOCKS + 1) // 2
    if L:
        for name in ("hT_ps", "hT_sb", "proj_ps", "table_sb"):
            st[name].base += BLOCKS
        st["w_ready"].base += 1
        for p in range(2):
            st[f"tb{p}"].base += 16 * (2 if L.extra else 1) * (even - p)
    st["variance"].base += norms * BLOCKS
    st["inv_std"].base += norms * BLOCKS
    st["w_in"].base += 16 * sb["n_w"]
    st["pre_done"].base += BLOCKS
    if n in (1, 2, 5, 6):
        st["exp_in"].base += BLOCKS
        st["exp_out"].base += BLOCKS
    for p in range(2):
        st[f"in{p}"].base += 16 * len(loads) * (even - p)
        st[f"out{p}"].base += 16 * len(stores) * (even - p)


def edge_pass(nc, st, io, sb, n):
    L = LAYERS[n]
    H, D, F = L.heads, L.depth, L.feat
    CW = L.acc
    GE = GROUP * P
    with ExitStack() as c:
        def tmp(name, shape, dt=F32):
            return c.enter_context(nc.sbuf_tensor(f"e{n}_{name}", shape, dt))

        rows = [[tmp(f"rows{p}_{s}", [P, CW]) for s in range(GROUP)] for p in range(2)]
        idx = tmp("idx", [P, 2, GROUP], I32)
        onehot = tmp("onehot", [P, 2, GROUP, P])
        onehot_T = tmp("onehot_T", [P, GROUP, P])
        er_edge = tmp("er_edge", [P, 2, GROUP + 1, H])
        el = tmp("el", [P, GROUP, H])
        pens = tmp("pens", [MAX_HEADS, 2, 2, GE], BF16)
        forward = tmp("forward", [MAX_HEADS, GE])
        top = tmp("top", [MAX_HEADS, GE + P])
        logit = tmp("logit", [P, 2 * GROUP + 2, H])
        diff = tmp("diff", [P, GROUP, H])
        weight = tmp("weight", [P, 2, GROUP, H])
        drop = tmp("drop", [P, H])
        rho = tmp("rho", [P, H])
        ps_el = c.enter_context(nc.psum_tensor(f"e{n}_ps_el", [P, GE], F32))
        ps_sum = [c.enter_context(nc.psum_tensor(f"e{n}_ps_sum{p}", [P, 1024], F32)) for p in range(2)]
        ps_turn = c.enter_context(nc.psum_tensor(f"e{n}_ps_turn", [P, 512], F32))
        ps_small = c.enter_context(nc.psum_tensor(f"e{n}_ps_small", [P, 512], F32))
        ps_er = ps_small[:, 0:GROUP * H].rearrange("p (s h) -> p s h", h=H)
        ps_top = ps_small[:, 128:128 + (GROUP + 1) * H].rearrange("p (s h) -> p s h", h=H)
        ps_rho = ps_small[:, 256:256 + H]
        blk = c.enter_context(nc.Block())

        def slots(fn, eng):
            fn(0, 0)
            fn(1, 1)
            with eng.Fori(0, (GROUPS - 2) // 2) as i:
                for p in range(2):
                    fn(2 * i + 2 + p, p)
            fn(GROUPS, 0)

        def is_last(g):
            return isinstance(g, int) and g >= GROUPS

        def is_first(g):
            return isinstance(g, int) and g == 0

        def round_of(g, p):
            return g - p

        @blk.sync
        def _(sp):
            def slot(g, p):
                if is_last(g):
                    return
                st["scanned"].wait(sp, g - 1)
                src = io["pen"][:, bass.ds(g * GE, GE)].unsqueeze(0).to_broadcast([H, 2, GE])
                sp.dma_start(pens[0:H, p, :, :], src).then_inc(st[f"pens{p}"].sem, 16)

            slots(slot, sp)

        @blk.gpsimd
        def _(pool):
            def slot(g, p):
                if is_last(g):
                    return
                st["idx_ready"].wait(pool, g + 1)
                st["summed"].wait(pool, GROUP * (g - 1))
                pool.sem_inc(st["gathering"].sem, 1)
                for s in range(GROUP):
                    nc.gpsimd.indirect_dma_start(
                        out=rows[p][s][:, 0:L.row], out_offset=None, in_=io[f"rows{n}"][:, :],
                        in_offset=bass.IndirectOffsetOnAxis(ap=idx[:, p, s:s + 1], axis=0)).then_inc(
                            st[f"rows{p}"].sem, 16)

            slots(slot, pool)

        @blk.vector
        def _(dve):
            v = nc.vector

            def indices(g, p):
                if not (isinstance(g, int) and g < 2):
                    st[f"rows{p}"].wait(dve, 8 * GROUP * (round_of(g, p)))
                v.tensor_copy(idx[:, p, :], sb["src_of"][:, bass.ds(g * GROUP, GROUP)]).then_inc(
                    st["idx_ready"].sem, 1)

            def onehots(g, p):
                st["summed"].wait(dve, GROUP * (g - 1))
                for s in range(GROUP):
                    v.tensor_scalar(onehot[:, p, s, :], sb["iota"][:, :],
                                    sb["dst_in_block"][:, bass.ds(g * GROUP + s, 1)], None, ALU.is_equal)
                v.drain().then_inc(st["onehot"].sem, 1)

            def source_logits(g, p):
                st[f"rows{p}"].wait(dve, 8 * GROUP * round_of(g, p) + 16 * GROUP)
                for s in range(GROUP):
                    r = rows[p][s][:, F:F + H]
                    if L.edge_term:
                        v.tensor_scalar(el[:, s, :], r, sb["edge_term"][:, bass.ds(g * GROUP + s, 1)], None, ALU.add)
                    else:
                        v.tensor_copy(el[:, s, :], r)
                v.drain().then_inc(st["el"].sem, 1)

            def scans(g, p):
                st[f"pens{p}"].wait(dve, 8 * round_of(g, p) + 16)
                st["el_ps"].wait(dve, g + 1)
                v.tensor_tensor_scan(forward[0:H, :], pens[0:H, p, 0, :], ps_el[0:H, :], sb["carry"][0:H, 0:1],
                                     ALU.add, ALU.max)
                v.tensor_scalar(top[0:H, GE:GE + P], sb["ones"][0:H, :], sb["carry"][0:H, 0:1], None, ALU.mult)
                v.drain()
                v.tensor_tensor_scan(top[0:H, GE - 1::-1], pens[0:H, p, 1, ::-1], forward[0:H, ::-1], LOW,
                                     ALU.add, ALU.max)
                v.tensor_copy(sb["carry"][0:H, 0:1], forward[0:H, GE - 1:GE])
                v.drain().then_inc(st["scanned"].sem, 1)

            def exponents(g, p):
                st["er_sb"].wait(dve, g + 1)
                st["top_ps"].wait(dve, g + 1)
                v.tensor_tensor(logit[:, GROUP:2 * GROUP, :], ps_top[:, 0:GROUP, :], er_edge[:, p, 0:GROUP, :],
                                ALU.add)
                v.tensor_tensor(logit[:, 2 * GROUP, :], ps_top[:, GROUP, :], er_edge[:, p, 0, :], ALU.add)
                v.tensor_tensor(logit[:, 0:GROUP, :], el[:, :, :], er_edge[:, p, 0:GROUP, :], ALU.add)
                if L.self_loop:
                    for s in range(GROUP):
                        v.tensor_scalar(rows[p][s][:, F + H:F + 2 * H], ps_top[:, s, :],
                                        sb["ends_here"][:, bass.ds(g * GROUP + s, 1)], None, ALU.mult)
                v.drain()
                v.scalar_tensor_tensor(logit[:, 0:2 * GROUP + 1, :], logit[:, 0:2 * GROUP + 1, :], L.slope,
                                       logit[:, 0:2 * GROUP + 1, :], ALU.mult, ALU.max)
                v.drain()
                v.tensor_tensor(diff[:, :, :], logit[:, 0:GROUP, :], logit[:, GROUP:2 * GROUP, :], ALU.subtract)
                v.tensor_tensor(drop[:, :], logit[:, 2 * GROUP, :], logit[:, GROUP, :], ALU.subtract)
                v.drain()
                v.tensor_scalar(drop[:, :], drop[:, :], sb["goes_on"][:, bass.ds(g, 1)], None, ALU.mult)
                v.drain().then_inc(st["exponents"].sem, 1)

            def message(g, p, s):
                if s == 0:
                    st["weights"].wait(dve, g + 1)
                R = rows[p][s]
                if H == 1:
                    v.tensor_scalar(R[:, 0:F], R[:, 0:F], weight[:, p, s, 0:1], None, ALU.mult)
                else:
                    v.tensor_tensor(per_head(R[:, 0:F], H), per_head(R[:, 0:F], H),
                                    weight[:, p, s, :].unsqueeze(2).to_broadcast([P, H, D]), ALU.mult)
                v.tensor_copy(R[:, F:F + H], weight[:, p, s, :])
                v.drain().then_inc(st["message"].sem, 1)

            def rescale(g, blocks):
                st["rho"].wait(dve, g + 1)
                A = sb["acc"][:, bass.ds(blocks[0] * CW, CW)]
                v.tensor_tensor(per_head(A[:, 0:F], H), per_head(A[:, 0:F], H),
                                rho[:, :].unsqueeze(2).to_broadcast([P, H, D]), ALU.mult)
                v.tensor_tensor(A[:, F:F + H], A[:, F:F + H], rho[:, :], ALU.mult)
                v.drain()

            def add(g, s, blocks):
                A = sb["acc"][:, bass.ds(blocks[s] * CW, CW)]
                st["summed"].wait(dve, GROUP * g + s + 1)
                v.tensor_tensor(A, A, ps_sum[s % 2][:, 0:CW], ALU.add)
                v.drain().then_inc(st["added"].sem, 1)

            def slot(g, p):
                u, q = g - 1, 1 - p
                if not is_first(g):
                    blocks = [v.value_load(sb["block_of"][0:1, bass.ds(u * GROUP + s, 1)], min_val=0,
                                           max_val=BLOCKS - 1) for s in range(GROUP)]
                if not is_last(g):
                    if is_first(g):
                        indices(0, 0)
                        indices(1, 1)
                    onehots(g, p)
                if not is_first(g):
                    rescale(u, blocks)
                    for s in range(4):
                        message(u, q, s)
                        if s >= 2:
                            add(u, s - 2, blocks)
                if not is_last(g):
                    source_logits(g, p)
                    if not (isinstance(g, int) and g < 1):
                        pass
                if not is_first(g):
                    for s in range(4, GROUP):
                        message(u, q, s)
                        add(u, s - 2, blocks)
                if not is_last(g):
                    scans(g, p)
                if not is_first(g):
                    for s in range(GROUP - 2, GROUP):
                        add(u, s, blocks)
                if not is_last(g):
                    exponents(g, p)
                    indices(g + 2, p)

            slots(slot, dve)

        @blk.tensor
        def _(pe):
            ident = sb["ident"]

            def slot(g, p):
                u, q = g - 1, 1 - p
                if not is_last(g):
                    blocks = [pe.value_load(sb["block_of"][0:1, bass.ds(g * GROUP + s, 1)], min_val=0,
                                            max_val=BLOCKS - 1) for s in range(GROUP)]
                    for half in range(2):
                        st["turned_sb"].wait(pe, 2 * g + half)
                        if half == 0:
                            st["onehot"].wait(pe, g + 1)
                        for k in range(4):
                            mm = nc.tensor.transpose(ps_turn[:, k * P:(k + 1) * P], onehot[:, p, 4 * half + k, :],
                                                     ident[:, :])
                        mm.then_inc(st["turned"].sem, 1)
                    st["rho"].wait(pe, g)
                    st["turned_sb"].wait(pe, 2 * g + 2)
                    for s in range(GROUP):
                        mm = nc.tensor.matmul(ps_er[:, s, :], onehot_T[:, s, :],
                                              sb["er"][:, bass.ds(blocks[s] * H, H)], start=True, stop=True)
                    mm.then_inc(st["er_ps"].sem, 1)

                def sums(s):
                    st["added"].wait(pe, GROUP * u + s - 1)
                    st["message"].wait(pe, GROUP * u + s + 1)
                    for lo in range(0, CW, 512):
                        hi = min(lo + 512, CW)
                        mm = nc.tensor.matmul(ps_sum[s % 2][:, lo:hi], onehot[:, q, s, :],
                                              rows[q][s][:, lo:hi], start=True, stop=True)
                    mm.then_inc(st["summed"].sem, 1)

                if not is_first(g):
                    for s in range(4):
                        sums(s)
                if not is_last(g):
                    st["scanned"].wait(pe, g)
                    st["el"].wait(pe, g + 1)
                    for s in range(GROUP):
                        mm = nc.tensor.transpose(ps_el[0:H, s * P:(s + 1) * P], el[:, s, :], ident[:, :])
                    mm.then_inc(st["el_ps"].sem, 1)
                if not is_first(g):
                    for s in range(4, GROUP):
                        sums(s)
                if not is_last(g):
                    st["er_sb"].wait(pe, g + 1)
                    st["scanned"].wait(pe, g + 1)
                    for s in range(GROUP + 1):
                        mm = nc.tensor.matmul(ps_top[:, s, :], top[0:H, s * P:(s + 1) * P], ident[0:H, 0:H],
                                              start=True, stop=True)
                    mm.then_inc(st["top_ps"].sem, 1)
                    st["exponents"].wait(pe, g + 1)
                    nc.tensor.matmul(ps_rho, onehot[:, p, 0, :], drop[:, :], start=True, stop=True).then_inc(
                        st["rho_ps"].sem, 1)

            slots(slot, pe)

        @blk.scalar
        def _(act):
            def slot(g, p):
                if is_last(g):
                    return
                for half in range(2):
                    if half == 0:
                        st["er_ps"].wait(act, g)
                    st["turned"].wait(act, 2 * g + half + 1)
                    nc.scalar.activation(onehot_T[:, 4 * half:4 * half + 4, :].rearrange("p s e -> p (s e)"),
                                         ps_turn[:, :], ACT.Copy).then_inc(st["turned_sb"].sem, 1)
                st["exponents"].wait(act, g - 1)
                st["er_ps"].wait(act, g + 1)
                nc.scalar.activation(er_edge[:, p, 0:GROUP, :], ps_er, ACT.Copy).then_inc(st["er_sb"].sem, 1)
                st["message"].wait(act, GROUP * (g - 1))
                st["exponents"].wait(act, g + 1)
                nc.scalar.activation(weight[:, p, :, :], diff[:, :, :], ACT.Exp).then_inc(st["weights"].sem, 1)
                st["rho_ps"].wait(act, g + 1)
                nc.scalar.activation(rho[:, :], ps_rho, ACT.Exp).then_inc(st["rho"].sem, 1)

            slots(slot, act)

    for name in ("scanned", "idx_ready", "gathering", "onehot", "el", "el_ps", "er_ps", "er_sb", "top_ps",
                 "exponents", "weights", "rho", "rho_ps"):
        st[name].base += GROUPS
    st["idx_ready"].base += 2
    for name in ("turned", "turned_sb"):
        st[name].base += 2 * GROUPS
    for name in ("message", "summed", "added"):
        st[name].base += GROUPS * GROUP
    for p in range(2):
        st[f"pens{p}"].base += 16 * GROUPS // 2
        st[f"rows{p}"].base += 16 * GROUP * GROUPS // 2


STAGES = ["variance", "inv_std", "w_in", "w_ready", "pre_done", "exp_in", "exp_out", "hT_ps", "hT_sb", "proj_ps", "table_sb",
          "in0", "in1", "out0", "out1", "tb0", "tb1",
          "scanned", "idx_ready", "gathering", "onehot", "el", "el_ps", "er_ps", "er_sb", "top_ps", "exponents",
          "weights", "rho", "rho_ps", "turned", "turned_sb", "message", "summed", "added",
          "pens0", "pens1", "rows0", "rows1"]


def build(nc, io):
    with ExitStack() as ctx:
        def keep(name, shape, dt=F32):
            return ctx.enter_context(nc.sbuf_tensor(name, shape, dt))

        sb = {
            "acc": keep("acc", [P, BLOCKS * MAX_ACC]),
            "er": keep("er", [P, BLOCKS * MAX_HEADS]),
            "src_of": keep("src_of", [P, STEPS + 2 * GROUP], I32),
            "dst_in_block": keep("dst_in_block", [P, STEPS]),
            "ends_here": keep("ends_here", [P, STEPS]),
            "edge_term": keep("edge_term", [P, STEPS]),
            "goes_on": keep("goes_on", [P, GROUPS]),
            "block_of": keep("block_of", [P, STEPS], I32),
            "ident": keep("ident", [P, P]),
            "iota": keep("iota", [P, P]),
            "ones": keep("ones", [P, P]),
            "carry": keep("carry", [P, 1]),
            "minus_half": keep("minus_half", [P, 1]),
        }
        st = {name: Stage(nc, ctx, name) for name in STAGES}

        def scratch(name, shape, dt=F32):
            return nc.dram_tensor("dram_" + name, shape, dt, kind="Internal").ap()

        NP = BLOCKS * P
        io["walk_rows"] = scratch("walk_rows", [STEP_ROWS * P * P + 2 * P], I32)
        io["walk_block"] = scratch("walk_block", [STEP_ROWS * P], I32)
        io["ea_flat"] = scratch("ea_flat", [P, TILES])
        io["ea_tiles"] = io["ea_flat"].rearrange("p j -> (p j)").rearrange("(t q) -> t q", q=P)
        io["pen"] = scratch("pen", [2, STEP_ROWS * P * P], BF16)
        io["x_mid"] = scratch("x_mid", [NP, DIM])
        io["h_mid"] = scratch("h_mid", [NP, DIM])
        io["hs_mid"] = scratch("hs_mid", [NP, DIM])
        for n, L in enumerate(LAYERS):
            io[f"rows{n}"] = scratch(f"rows_table{n}", [NP, L.row])

        with nc.Block() as blk:
            @blk.vector
            def _(dve):
                nc.vector.memset(sb["ones"][:, :], 1.0)
                nc.vector.memset(sb["minus_half"][:, :], -0.5)
                nc.vector.memset(sb["src_of"][:, STEPS:], 0)
        prepare(nc, ctx, st, io, {**sb, "src_of": sb["src_of"][:, 0:STEPS]})
        for n in range(len(LAYERS) + 1):
            node_phase(nc, st, io, sb, n)
            if n < len(LAYERS):
                edge_pass(nc, st, io, sb, n)


def kernel(**inputs):
    import numpy as np
    import concourse.bacc as bacc
    from concourse import mybir as mb
    from concourse.bass_utils import run_bass_kernel_spmd as run

    x = {k: np.asarray(v) for k, v in inputs.items()}
    NP, EP = BLOCKS * P, TILES * P

    def pad(a, rows, fill):
        out = np.full((rows,) + a.shape[1:], fill, a.dtype)
        out[:a.shape[0]] = a
        return out

    dst = pad(x["dst"], EP, NO_NODE)
    arrays = {
        "x": pad(x["x"], NP, 0),
        "src_tiles": pad(x["src"], EP, 0).reshape(TILES, P),
        "dst_tiles": dst.reshape(TILES, P),
        "dst_last": np.ascontiguousarray(dst.reshape(TILES, P)[:TILES - 1, P - 1]),
        "edge_attr": pad(x["edge_attr_64"], EP, 0).reshape(P, TILES * EDGE_DIM),
        "iota": np.arange(512, dtype=np.float32),
        "step_no": np.arange(STEP_ROWS * P, dtype=np.float32).reshape(STEP_ROWS, P).T.copy(),
        "ident": np.eye(P, dtype=np.float32),
        "no_node": np.full((P,), -1, np.int32),
        "att": x["L2_gnn_W_att"].reshape(-1),
        "gamma": x["L0_gnn_gamma"], "beta": x["L0_gnn_beta"],
        "b1": x["L3_gnn_b1"], "b2": x["L3_gnn_b2"], "prelu": x["L3_gnn_prelu_w"].reshape(1),
        "w0": x["L0_gnn_W"], "w1": x["L1_gnn_W1"], "w2": x["L1_gnn_W2"],
        "w3": np.concatenate([x["L2_gnn_W_func"].T, x["L2_gnn_W_self"].T], axis=1),
        "w4": x["L3_gnn_W1"], "w5": x["L3_gnn_W2"],
        "a0": np.stack([x["L0_gnn_a_src"].reshape(-1), x["L0_gnn_a_dst"].reshape(-1)]),
        "a1": np.stack([x["L1_gnn_attn_l1"].reshape(-1), x["L1_gnn_attn_r1"].reshape(-1)]),
        "a2": np.stack([x["L1_gnn_attn_l2"].reshape(-1), x["L1_gnn_attn_r2"].reshape(-1)]),
        "a3": x["L2_gnn_W_att"].reshape(-1)[:2 * DIM].reshape(2, DIM),
        "a4": np.stack([x["L3_gnn_a_src1"].reshape(-1), x["L3_gnn_a_dst1"].reshape(-1)]),
        "a5": np.stack([x["L3_gnn_a_src2"].reshape(-1), x["L3_gnn_a_dst2"].reshape(-1)]),
    }
    arrays = {"in_" + k: np.ascontiguousarray(v) for k, v in arrays.items()}
    nc = bacc.Bacc("TRN2", target_bir_lowering=False, num_devices=1)
    io = {k[3:]: nc.dram_tensor(k, v.shape, mb.dt.from_np(v.dtype), kind="ExternalInput").ap() for k, v in arrays.items()}
    io["out"] = nc.dram_tensor("out", (NP, DIM), mb.dt.float32, kind="ExternalOutput").ap()
    build(nc, io)
    r = run(nc, [arrays], core_ids=[0])
    return r.results[0]["out"][:NODES]
```

```python
from contextlib import ExitStack

import concourse.bass as bass
import concourse.mybir as mybir

F32 = mybir.dt.float32
BF16 = mybir.dt.bfloat16
I32 = mybir.dt.int32
U8 = mybir.dt.uint8
ALU = mybir.AluOpType
ACT = mybir.ActivationFunctionType
AX_X = mybir.AxisListType.X

P = 128
NODES = 3125
EDGES = 50000
DIM = 256
EDGE_DIM = 64
BLOCKS = -(-NODES // P)
TILES = -(-EDGES // P)
UNIT = 2
UNITS = -(-TILES // UNIT)
UE = UNIT * P
GROUP_UNITS = 4
GROUP = GROUP_UNITS * UNIT
GROUPS = -(-(UNITS + BLOCKS - 1) // GROUP_UNITS)
WALK = GROUPS * GROUP_UNITS
STEPS = GROUPS * GROUP
WALK_ROWS = -(-WALK // P)
NO_NODE = 4095
LN_EPS = 1e-5
LOW = -1e30
TINY = 1e-30
MAX_HEADS = 8
MAX_ACC = 528


class Stage:

    def __init__(self, nc, ctx, name):
        self.sem = ctx.enter_context(nc.semaphore(name))
        self.base = 0

    def wait(self, eng, count):
        if isinstance(count, int) and count <= 0:
            return
        eng.wait_ge(self.sem, self.base + count)


class Layer:

    def __init__(self, heads, depth, k, slope, self_loop=False, edge_term=False, extra=0):
        self.heads, self.depth, self.k, self.slope = heads, depth, k, slope
        self.self_loop, self.edge_term, self.extra = self_loop, edge_term, extra
        self.feat = heads * depth
        self.row = self.feat + heads
        self.acc = self.feat + (2 if self_loop else 1) * heads
        self.proj = self.feat + 2 * heads + extra
        self.chunks = k // P


LAYERS = [
    Layer(8, 32, 256, 0.2),
    Layer(8, 64, 256, 0.2),
    Layer(1, 256, 512, 0.2),
    Layer(1, 256, 256, 0.01, edge_term=True, extra=256),
    Layer(4, 128, 256, 0.2, self_loop=True),
    Layer(1, 256, 512, 0.2, self_loop=True),
]


def per_head(ap, heads):
    return ap.rearrange("p (h d) -> p h d", h=heads)


def looped(fn, eng, count):
    fn(0, 0)
    fn(1, 1)
    with eng.Fori(0, (count - 2) // 2) as i:
        for p in range(2):
            fn(2 * i + 2 + p, p)
    if count % 2:
        fn(count - 1, 0)


def prepare(nc, ctx, st, io, sb):
    row_of = io["walk_rows"]
    W = WALK_ROWS * P * UE
    with ExitStack() as c:
        def tmp(name, shape, dt=F32):
            return c.enter_context(nc.sbuf_tensor(name, shape, dt))

        def sem(name):
            return c.enter_context(nc.semaphore(name))

        last = tmp("last_dst", [P, UNITS - 1], I32)
        leave = tmp("leave_step", [P, UNITS - 1])
        iota_units = tmp("iota_units", [P, UNITS - 1])
        passed = tmp("passed", [P, UNITS - 1])
        step_no = tmp("step_no", [P, WALK_ROWS])
        unit_f = tmp("unit_f", [P, WALK_ROWS])
        unit_i = tmp("unit_i", [P, WALK_ROWS], I32)
        block_f = tmp("block_f", [P, WALK_ROWS])
        block_i = tmp("block_i", [P, WALK_ROWS], I32)
        src_rows = tmp("src_rows", [P, WALK_ROWS, UE], I32)
        dst_rows = tmp("dst_rows", [P, WALK_ROWS, UE], I32)
        dst_before = tmp("dst_before", [P, WALK_ROWS, UE], I32)
        dst_after = tmp("dst_after", [P, WALK_ROWS, UE], I32)
        ea_rows = tmp("ea_rows", [P, WALK_ROWS, UE])
        src_f = tmp("src_f", [P, WALK_ROWS, UE])
        dst_f = tmp("dst_f", [P, WALK_ROWS, UE])
        dst_bf = tmp("dst_bf", [P, WALK_ROWS, UE], BF16)
        starts = tmp("starts", [P, WALK_ROWS, UE])
        ends = tmp("ends", [P, WALK_ROWS, UE])
        pen = tmp("pen", [P, 2, WALK_ROWS, UE], BF16)
        goes = tmp("goes", [P, GROUPS])
        att_e = tmp("att_e", [P, EDGE_DIM])
        EPP = UNITS * UNIT
        NCH = 4
        CH = -(-EPP // NCH)
        ea_in = tmp("ea_in", [P, 2, CH * EDGE_DIM])
        ea_out = tmp("ea_out", [P, EPP])
        psum = [c.enter_context(nc.psum_tensor(f"turn{k}", [P, 512], F32)) for k in range(5)]

        s_in, s_att, s_t, s_b, s_ea_st, s_seq, s_sh, s_bi = (sem(n) for n in (
            "prep_in", "att_in", "unit_index", "block_store", "ea_store", "walk_dst_store", "shifted", "block_row"))
        s_eain = [sem("ea_in0"), sem("ea_in1")]
        s_g = [sem("src_got"), sem("dst_got"), sem("ea_got")]
        s_eadone, s_walk, s_mark, s_pen, s_turned, s_dve = (sem(n) for n in (
            "ea_chunk_done", "walk_f_ready", "marks_ready", "pen_store", "tables_turned", "prep_done"))
        blk = c.enter_context(nc.Block())

        @blk.sync
        def _(sp):
            sp.dma_start(last[:, :], io["dst_last"].partition_broadcast(P)).then_inc(s_in, 16)
            sp.dma_start(iota_units[:, :], io["iota"][0:UNITS - 1].partition_broadcast(P)).then_inc(s_in, 16)
            sp.dma_start(step_no[:, :], io["step_no"][:, :]).then_inc(s_in, 16)
            sp.dma_start(sb["ident"][:, :], io["ident"][:, :]).then_inc(s_in, 16)
            sp.dma_start(sb["iota"][:, :], io["iota"][0:P].partition_broadcast(P)).then_inc(s_in, 16)
            sp.dma_start(sb["lane"][:, :], io["lane"][:, :]).then_inc(s_in, 16)
            sp.dma_start(att_e[:, :], io["att"][2 * DIM:2 * DIM + EDGE_DIM].partition_broadcast(P)).then_inc(s_att, 16)
            for n in range(NCH):
                w = min(CH, EPP - n * CH)
                if n >= 2:
                    sp.wait_ge(s_eadone, n - 1)
                sp.dma_start(ea_in[:, n % 2, 0:w * EDGE_DIM],
                             io["edge_attr"][:, n * CH * EDGE_DIM:(n * CH + w) * EDGE_DIM]).then_inc(s_eain[n % 2], 16)
            sp.wait_ge(s_eadone, NCH)
            sp.dma_start(io["ea_flat"][:, :], ea_out[:, :]).then_inc(s_ea_st, 16)

        @blk.scalar
        def _(act):
            act.wait_ge(s_t, 2)
            with nc.allow_non_contiguous_dma(reason="one number per unit"):
                act.dma_start(io["walk_block"].rearrange("(k p) -> p k", p=P), block_i[:, :]).then_inc(s_b, 16)
            act.wait_ge(s_b, 16)
            act.dma_start(sb["block_of"][0:1, :], io["walk_block"][0:WALK].unsqueeze(0)).then_inc(s_bi, 16)
            act.wait_ge(s_g[1], 16 * WALK_ROWS)
            seq = row_of[P:P + W].rearrange("(k p q) -> p k q", p=P, q=UE)
            act.dma_start(seq, dst_rows[:, :, :]).then_inc(s_seq, 16)
            act.dma_start(row_of[0:P].unsqueeze(0), io["no_node"].unsqueeze(0)).then_inc(s_seq, 16)
            act.dma_start(row_of[P + W:2 * P + W].unsqueeze(0), io["no_node"].unsqueeze(0)).then_inc(s_seq, 16)
            act.wait_ge(s_seq, 48)
            for buf, off in ((dst_before, P - 1), (dst_after, P + 1)):
                view = row_of[off:off + W].rearrange("(k p q) -> p k q", p=P, q=UE)
                act.dma_start(buf[:, :, :], view).then_inc(s_sh, 16)
            act.wait_ge(s_walk, 1)
            act.dma_start(io["dst_local"].rearrange("(k p q) -> p k q", p=P, q=UE), dst_bf[:, :, :]).then_inc(s_pen, 16)
            act.wait_ge(s_mark, 1)
            for d in range(2):
                view = io["pen"][d].rearrange("(k p q) -> p k q", p=P, q=UE)
                act.dma_start(view, pen[:, d, :, :]).then_inc(s_pen, 16)
            act.wait_ge(s_pen, 48)
            act.wait_ge(s_bi, 16)

        @blk.gpsimd
        def _(pool):
            pool.wait_ge(s_t, 1)
            for k in range(WALK_ROWS):
                for buf, table, s in ((src_rows, "src_units", s_g[0]), (dst_rows, "dst_units", s_g[1])):
                    nc.gpsimd.indirect_dma_start(
                        out=buf[:, k, :], out_offset=None, in_=io[table][:, :],
                        in_offset=bass.IndirectOffsetOnAxis(ap=unit_i[:, k:k + 1], axis=0)).then_inc(s, 16)
            pool.wait_ge(s_ea_st, 16)
            for k in range(WALK_ROWS):
                nc.gpsimd.indirect_dma_start(
                    out=ea_rows[:, k, :], out_offset=None, in_=io["ea_units"][:, :],
                    in_offset=bass.IndirectOffsetOnAxis(ap=unit_i[:, k:k + 1], axis=0)).then_inc(s_g[2], 16)

        @blk.vector
        def _(dve):
            v = nc.vector
            dve.wait_ge(s_in, 96)
            v.tensor_scalar(last[:, :], last[:, :], 7, None, ALU.arith_shift_right)
            v.drain()
            v.tensor_tensor(leave[:, :], last[:, :], iota_units[:, :], ALU.add)
            v.drain()
            for k in range(WALK_ROWS):
                v.tensor_scalar(passed[:, :], leave[:, :], step_no[:, k:k + 1], None, ALU.is_lt)
                v.drain()
                v.tensor_reduce(unit_f[:, k:k + 1], passed[:, :], AX_X, ALU.add)
                v.drain()
            v.tensor_copy(unit_i[:, :], unit_f[:, :]).then_inc(s_t, 1)
            v.tensor_tensor(block_f[:, :], step_no[:, :], unit_f[:, :], ALU.subtract)
            v.drain()
            v.tensor_scalar(block_i[:, :], block_f[:, :], float(BLOCKS - 1), None, ALU.min).then_inc(s_t, 1)
            v.tensor_scalar(block_f[:, :], block_f[:, :], float(P), None, ALU.mult)
            dve.wait_ge(s_att, 16)
            for n in range(NCH):
                w = min(CH, EPP - n * CH)
                dve.wait_ge(s_eain[n % 2], 16 * (n // 2 + 1))
                view = ea_in[:, n % 2, 0:w * EDGE_DIM].rearrange("p (j d) -> p j d", d=EDGE_DIM)
                v.tensor_tensor(view, view, att_e[:, :].unsqueeze(1).to_broadcast([P, w, EDGE_DIM]), ALU.mult)
                v.drain()
                v.tensor_reduce(ea_out[:, n * CH:n * CH + w], view, AX_X, ALU.add).then_inc(s_eadone, 1)
            dve.wait_ge(s_g[0], 16 * WALK_ROWS)
            dve.wait_ge(s_g[1], 16 * WALK_ROWS)
            v.tensor_copy(src_f[:, :, :], src_rows[:, :, :])
            for k in range(WALK_ROWS):
                v.tensor_scalar(dst_f[:, k, :], dst_rows[:, k, :], block_f[:, k:k + 1], None, ALU.subtract)
                v.tensor_scalar(dst_bf[:, k, :], dst_rows[:, k, :], block_f[:, k:k + 1], None, ALU.subtract)
            v.drain().then_inc(s_walk, 1)
            dve.wait_ge(s_sh, 32)
            v.tensor_tensor(starts[:, :, :], dst_rows[:, :, :], dst_before[:, :, :], ALU.not_equal)
            v.tensor_tensor(ends[:, :, :], dst_rows[:, :, :], dst_after[:, :, :], ALU.not_equal)
            v.drain()
            v.tensor_scalar(pen[:, 0, :, :], starts[:, :, :], LOW, None, ALU.mult)
            v.tensor_scalar(pen[:, 1, :, :], ends[:, :, :], LOW, None, ALU.mult)
            v.drain().then_inc(s_mark, 1)
            for n, dst in enumerate((sb["src_of"], sb["dst_in_block"], sb["ends_here"], None, sb["edge_term"])):
                dve.wait_ge(s_turned, n + 1)
                by_half = psum[n][:, :].rearrange("p (j u) -> p j u", j=UNIT)
                if dst is None:
                    v.tensor_copy(goes[:, :], by_half[:, 0, 0:WALK:GROUP_UNITS])
                else:
                    for j in range(UNIT):
                        v.tensor_copy(dst[:, j:STEPS:UNIT], by_half[:, j, 0:WALK])
            v.drain()
            v.tensor_scalar(goes[:, :], goes[:, :], -1.0, 1.0, ALU.mult, ALU.add)
            v.drain()
            v.tensor_scalar(sb["goes_on"][:, :], goes[:, :], sb["ident"][:, 0:1], None, ALU.mult)
            v.drain().then_inc(s_dve, 1)

        @blk.tensor
        def _(pe):
            pe.wait_ge(s_in, 96)
            for n, rows in enumerate((src_f, dst_f, ends, starts, ea_rows)):
                if n == 0:
                    pe.wait_ge(s_walk, 1)
                if n == 2:
                    pe.wait_ge(s_mark, 1)
                if n == 4:
                    pe.wait_ge(s_g[2], 16 * WALK_ROWS)
                for k in range(WALK_ROWS):
                    for j in range(UNIT):
                        at = (j * WALK_ROWS + k) * P
                        mm = nc.tensor.transpose(psum[n][:, at:at + P], rows[:, k, j * P:(j + 1) * P],
                                                 sb["ident"][:, :])
                mm.then_inc(s_turned, 1)


def make_onehots(nc, st, io, sb):
    GE = GROUP * P
    with ExitStack() as c:
        rows = c.enter_context(nc.sbuf_tensor("dst_bcast", [P, 2, GE], BF16))
        flat = c.enter_context(nc.sbuf_tensor("onehot_bytes", [P, 2, GROUP, P], U8))
        blk = c.enter_context(nc.Block())

        @blk.sync
        def _(sp):
            def slot(g, p):
                st["oh_used"].wait(sp, g - 1)
                sp.dma_start(rows[:, p, :], io["dst_local"][bass.ds(g * GE, GE)].partition_broadcast(P)).then_inc(
                    st[f"oh_in{p}"].sem, 16)

            looped(slot, sp, GROUPS)

        @blk.vector
        def _(dve):
            v = nc.vector

            def slot(g, p):
                if isinstance(g, int):
                    st[f"oh_out{p}"].wait(dve, 16 * (g // 2))
                else:
                    st[f"oh_out{p}"].wait(dve, 8 * (g - p))
                for s in range(GROUP):
                    v.tensor_scalar(flat[:, p, s, :], sb["iota"][:, :],
                                    sb["dst_in_block"][:, bass.ds(g * GROUP + s, 1)], None, ALU.is_equal)
                st[f"oh_in{p}"].wait(dve, 8 * (g - p) + 16)
                v.tensor_scalar(sb["onehot_T"][:, bass.ds(g * GE, GE)], rows[:, p, :], sb["lane"][:, 0:1], None,
                                ALU.is_equal).then_inc(st["oh_used"].sem, 1)

            looped(slot, dve, GROUPS)

        @blk.scalar
        def _(act):
            def slot(g, p):
                st["oh_used"].wait(act, g + 1)
                act.dma_start(io["onehot"][bass.ds(g * P, P), :],
                              flat[:, p, :, :].rearrange("p s d -> p (s d)")).then_inc(st[f"oh_out{p}"].sem, 16)

            looped(slot, act, GROUPS)
            for p in range(2):
                st[f"oh_out{p}"].wait(act, 16 * ((GROUPS + 1 - p) // 2))


def node_phase(nc, st, io, sb, n):
    L = LAYERS[n] if n < len(LAYERS) else None
    prev = LAYERS[n - 1] if n else None
    loads = {0: ["x"], 1: ["h"], 2: [], 3: ["x"], 4: ["x", "h", "hs"], 5: ["table"], 6: ["x", "table"]}[n]
    if n == 1:
        loads = ["x", "h"]
    stores = {0: ["h"], 1: ["x"], 2: [], 3: ["x", "h"], 4: ["x"], 5: [], 6: ["out"]}[n]
    with ExitStack() as c:
        def tmp(name, shape, dt=F32):
            return c.enter_context(nc.sbuf_tensor(f"n{n}_{name}", shape, dt))

        width = {"x": DIM, "h": DIM, "hs": DIM, "table": prev.row if prev else 0}
        tin = {name: tmp("in_" + name, [P, 2, width[name]]) for name in loads}
        xo = tmp("x_out", [P, 2, DIM])
        k_in = L.k if L else DIM
        h = tmp("h", [P, 2, 512])
        a = tmp("a", [P, 512])
        b = tmp("b", [P, 512])
        e = tmp("e", [P, 512])
        small = tmp("small", [P, 96])
        vec = tmp("vec", [P, 2, 512])
        vec1 = tmp("vec1", [P, 1])
        psum_t = [c.enter_context(nc.psum_tensor(f"n{n}_ps_hT{p}", [P, 512], F32)) for p in range(2)]
        psum_f = [c.enter_context(nc.psum_tensor(f"n{n}_ps_proj{p}", [P, 1024], F32)) for p in range(2)]
        if L:
            wx = tmp("wx", [P, L.chunks, L.proj])
            wtmp = tmp("wtmp", [P, 512])
            avec = tmp("avec", [P, 2, L.feat])
            hT = tmp("hT", [P, 2, 512])
            tb = tmp("tb", [P, 2, L.row + L.extra])
        split = min(512, L.proj) if L else 0
        if L and L.extra:
            split = L.feat + 2 * L.heads
        blk = c.enter_context(nc.Block())

        dram = {"x": io["x"] if n <= 1 else io["x_mid"], "h": io["h_mid"], "hs": io["hs_mid"],
                "table": io[f"rows{n - 1}"] if n else None}
        sto = {"x": io["x_mid"], "h": io["h_mid"], "out": io["out"]}

        def rows(t):
            return bass.ds(t * P, P)

        def slots(fn, eng):
            fn(0, 0)
            fn(1, 1)
            with eng.Fori(0, (BLOCKS - 3) // 2) as i:
                for p in range(2):
                    fn(2 * i + 2 + p, p)
            for t in range(BLOCKS - 1, BLOCKS + 1):
                fn(t, t % 2)

        @blk.sync
        def _(sp):
            nw = 0
            if L:
                wsrc = io[f"w{n}"]
                for k in range(L.chunks):
                    sp.dma_start(wx[:, k, 0:L.feat], wsrc[k * P:(k + 1) * P, 0:L.feat]).then_inc(st["w_in"].sem, 16)
                    if L.extra:
                        sp.dma_start(wx[:, k, L.feat + 2 * L.heads:], wsrc[k * P:(k + 1) * P, L.feat:]).then_inc(
                            st["w_in"].sem, 16)
                    nw += 2 if L.extra else 1
                for j in range(2):
                    sp.dma_start(avec[:, j, :], io[f"a{n}"][j].partition_broadcast(P)).then_inc(st["w_in"].sem, 16)
                    nw += 1
            if n == 1:
                sp.dma_start(vec[:, 0, 0:DIM], io["gamma"].partition_broadcast(P)).then_inc(st["w_in"].sem, 16)
                sp.dma_start(vec[:, 1, 0:DIM], io["beta"].partition_broadcast(P)).then_inc(st["w_in"].sem, 16)
                nw += 2
            if n == 5:
                sp.dma_start(vec[:, 0, :], io["b1"].partition_broadcast(P)).then_inc(st["w_in"].sem, 16)
                sp.dma_start(vec1[:, :], io["prelu"].partition_broadcast(P)).then_inc(st["w_in"].sem, 16)
                nw += 2
            if n == 6:
                sp.dma_start(vec[:, 0, 0:DIM], io["b2"].partition_broadcast(P)).then_inc(st["w_in"].sem, 16)
                nw += 1
            sb["n_w"] = nw

            def load(t, p):
                st["pre_done"].wait(sp, t - 1)
                for name in loads:
                    sp.dma_start(tin[name][:, p, :], dram[name][rows(t), 0:width[name]]).then_inc(
                        st[f"in{p}"].sem, 16)

            def slot(t, p):
                if not (isinstance(t, int) and t >= BLOCKS) and loads:
                    load(t, p)
                if not (isinstance(t, int) and t == 0):
                    u, q = t - 1, 1 - p
                    if stores:
                        st["pre_done"].wait(sp, u + 1)
                    for name in stores:
                        src = {"x": xo, "out": xo, "h": h}[name]
                        sp.dma_start(sto[name][rows(u), 0:DIM], src[:, q, 0:DIM]).then_inc(st[f"out{q}"].sem, 16)
                    if L:
                        st["table_sb"].wait(sp, u + 1)
                        sp.dma_start(io[f"rows{n}"][rows(u), 0:L.row], tb[:, q, 0:L.row]).then_inc(st[f"tb{q}"].sem, 16)
                        if L.extra:
                            sp.dma_start(io["hs_mid"][rows(u), :], tb[:, q, L.row:]).then_inc(st[f"tb{q}"].sem, 16)

            slots(slot, sp)
            for p in range(2):
                tiles = (BLOCKS + 1 - p) // 2
                if stores:
                    st[f"out{p}"].wait(sp, 16 * tiles * len(stores))
                if L:
                    st[f"tb{p}"].wait(sp, 16 * tiles * (2 if L.extra else 1))

        @blk.vector
        def _(dve):
            v = nc.vector
            st["w_in"].wait(dve, 16 * sb["n_w"])
            if L:
                for k in range(L.chunks):
                    for j in range(2):
                        v.tensor_tensor(wtmp[:, 0:L.feat], wx[:, k, 0:L.feat], avec[:, j, :], ALU.mult)
                        v.drain()
                        v.tensor_reduce(wx[:, k, L.feat + j * L.heads:L.feat + (j + 1) * L.heads],
                                        per_head(wtmp[:, 0:L.feat], L.heads), AX_X, ALU.add)
                        v.drain()
                v.drain().then_inc(st["w_ready"].sem, 1)

            def norm(dst, src, count, relu=True):
                v.bn_stats(small[:, 0:6], src)
                v.drain()
                v.bn_aggr(small[:, 6:8], small[:, 0:6])
                v.drain()
                v.tensor_scalar(small[:, 8:9], small[:, 7:8], LN_EPS, None, ALU.add)
                v.tensor_scalar(dst, src, small[:, 6:7], 0.0 if relu else None, ALU.subtract,
                                ALU.max if relu else ALU.bypass)
                v.drain().then_inc(st["variance"].sem, 1)
                st["inv_std"].wait(dve, count)
                v.tensor_scalar(dst, dst, small[:, 9:10], None, ALU.mult)
                v.drain()

            def exp_of(t, width_):
                v.tensor_scalar(e[:, 0:width_], a[:, 0:width_], 0.0, None, ALU.min)
                v.drain().then_inc(st["exp_in"].sem, 1)
                st["exp_out"].wait(dve, t + 1)

            def sums(t):
                return sb["acc"][:, bass.ds(t * prev.acc, prev.acc)]

            def divide(dst, t):
                A = sums(t)
                H, F = prev.heads, prev.feat
                v.tensor_scalar(small[:, 16:16 + H], A[:, F:F + H], TINY, None, ALU.max)
                v.drain()
                v.reciprocal(small[:, 24:24 + H], small[:, 16:16 + H])
                v.drain()
                v.tensor_tensor(per_head(dst, H), per_head(A[:, 0:F], H),
                                small[:, 24:24 + H].unsqueeze(2).to_broadcast([P, H, prev.depth]), ALU.mult)
                v.drain()

            def join_self(t, p):
                A = sums(t)
                H, F, D = prev.heads, prev.feat, prev.depth
                own = tin["table"]
                er = sb["er"][:, bass.ds(t * H, H)]
                den, top = A[:, F:F + H], A[:, F + H:F + 2 * H]
                s = lambda i, m=1: small[:, 16 + 8 * i:16 + 8 * i + m * H]
                v.tensor_scalar(s(0), den, 0.5, None, ALU.is_lt)
                v.drain()
                v.scalar_tensor_tensor(s(1), s(0), LOW, top, ALU.mult, ALU.add)
                v.drain()
                v.tensor_tensor(s(2), s(1), own[:, p, F:F + H], ALU.max)
                v.drain()
                v.tensor_tensor(s(1), s(1), er, ALU.add)
                v.tensor_tensor(s(2), s(2), er, ALU.add)
                v.tensor_tensor(s(3), own[:, p, F:F + H], er, ALU.add)
                v.drain()
                for i in (1, 2, 3):
                    v.scalar_tensor_tensor(s(i), s(i), prev.slope, s(i), ALU.mult, ALU.max)
                v.drain()
                v.tensor_tensor(e[:, 0:H], s(1), s(2), ALU.subtract)
                v.tensor_tensor(e[:, H:2 * H], s(3), s(2), ALU.subtract)
                v.drain().then_inc(st["exp_in"].sem, 1)
                st["exp_out"].wait(dve, t + 1)
                v.tensor_tensor(s(4), den, e[:, 0:H], ALU.mult)
                v.tensor_tensor(per_head(a[:, 0:F], H), per_head(A[:, 0:F], H),
                                e[:, 0:H].unsqueeze(2).to_broadcast([P, H, D]), ALU.mult)
                v.tensor_tensor(per_head(b[:, 0:F], H), per_head(own[:, p, 0:F], H),
                                e[:, H:2 * H].unsqueeze(2).to_broadcast([P, H, D]), ALU.mult)
                v.drain()
                v.tensor_tensor(s(4), s(4), e[:, H:2 * H], ALU.add)
                v.tensor_tensor(a[:, 0:F], a[:, 0:F], b[:, 0:F], ALU.add)
                v.drain()
                v.reciprocal(s(5), s(4))
                v.drain()
                v.tensor_tensor(per_head(a[:, 0:F], H), per_head(a[:, 0:F], H),
                                s(5).unsqueeze(2).to_broadcast([P, H, D]), ALU.mult)
                v.drain()

            def slot(t, p):
                if isinstance(t, int) and t >= BLOCKS:
                    return
                if L:
                    st["hT_ps"].wait(dve, t - 1)
                if stores:
                    if isinstance(t, int):
                        st[f"out{p}"].wait(dve, 16 * len(stores) * (t // 2))
                    else:
                        st[f"out{p}"].wait(dve, 8 * len(stores) * (t - p))
                if loads:
                    if isinstance(t, int):
                        st[f"in{p}"].wait(dve, 16 * len(loads) * (t // 2 + 1))
                    else:
                        st[f"in{p}"].wait(dve, 8 * len(loads) * (t - p) + 16 * len(loads))
                x_in = tin["x"][:, p, :] if "x" in tin else None
                xn, hn = xo[:, p, :], h[:, p, 0:DIM]
                if n == 0:
                    norm(hn, x_in, t + 1)
                elif n == 1:
                    divide(a[:, 0:DIM], t)
                    v.tensor_tensor(a[:, 0:DIM], a[:, 0:DIM], tin["h"][:, p, :], ALU.add)
                    v.drain()
                    norm(b[:, 0:DIM], a[:, 0:DIM], 2 * t + 1, relu=False)
                    v.tensor_tensor(b[:, 0:DIM], b[:, 0:DIM], vec[:, 0, 0:DIM], ALU.mult)
                    v.drain()
                    v.tensor_tensor(a[:, 0:DIM], b[:, 0:DIM], vec[:, 1, 0:DIM], ALU.add)
                    v.drain()
                    exp_of(t, DIM)
                    v.scalar_tensor_tensor(b[:, 0:DIM], e[:, 0:DIM], -1.0, x_in, ALU.add, ALU.add)
                    v.drain()
                    v.scalar_tensor_tensor(xn, a[:, 0:DIM], 0.0, b[:, 0:DIM], ALU.max, ALU.add)
                    v.drain()
                    norm(hn, xn, 2 * t + 2)
                elif n == 2:
                    divide(a[:, :], t)
                    exp_of(t, 512)
                    v.tensor_scalar(b[:, :], e[:, :], -1.0, None, ALU.add)
                    v.drain()
                    v.scalar_tensor_tensor(h[:, p, :], a[:, :], 0.0, b[:, :], ALU.max, ALU.add)
                    v.drain()
                elif n == 3:
                    divide(a[:, 0:DIM], t)
                    v.tensor_tensor(xn, a[:, 0:DIM], x_in, ALU.add)
                    v.drain()
                    norm(hn, xn, t + 1)
                elif n == 4:
                    divide(a[:, 0:DIM], t)
                    hp = tin["h"][:, p, :]
                    v.tensor_tensor(a[:, 0:DIM], a[:, 0:DIM], tin["hs"][:, p, :], ALU.add)
                    v.tensor_scalar(small[:, 32:33], sums(t)[:, DIM:DIM + 1], 0.5, None, ALU.is_gt)
                    v.tensor_scalar(small[:, 33:34], sums(t)[:, DIM:DIM + 1], 0.5, None, ALU.is_lt)
                    v.drain()
                    v.tensor_scalar(a[:, 0:DIM], a[:, 0:DIM], small[:, 32:33], None, ALU.mult)
                    v.drain()
                    v.scalar_tensor_tensor(a[:, 0:DIM], hp, small[:, 33:34], a[:, 0:DIM], ALU.mult, ALU.add)
                    v.drain()
                    v.scalar_tensor_tensor(b[:, 0:DIM], a[:, 0:DIM], 0.0, hp, ALU.max, ALU.add)
                    v.drain()
                    v.tensor_tensor(xn, b[:, 0:DIM], x_in, ALU.add)
                    v.drain()
                    norm(hn, xn, t + 1)
                elif n == 5:
                    join_self(t, p)
                    v.tensor_tensor(a[:, :], a[:, :], vec[:, 0, :], ALU.add)
                    v.drain()
                    v.tensor_scalar(b[:, :], a[:, :], 0.0, vec1[:, 0:1], ALU.min, ALU.mult)
                    v.drain()
                    v.scalar_tensor_tensor(h[:, p, :], a[:, :], 0.0, b[:, :], ALU.max, ALU.add)
                    v.drain()
                elif n == 6:
                    join_self(t, p)
                    v.tensor_tensor(a[:, 0:DIM], a[:, 0:DIM], vec[:, 0, 0:DIM], ALU.add)
                    v.drain()
                    v.tensor_tensor(xn, a[:, 0:DIM], x_in, ALU.add)
                v.drain().then_inc(st["pre_done"].sem, 1)

            slots(slot, dve)
            if L:
                for b0 in range(0, BLOCKS * L.acc, 4096):
                    v.memset(sb["acc"][:, b0:min(b0 + 4096, BLOCKS * L.acc)], 0.0)
                v.memset(sb["carry"][:, :], 0.0)

        norms = {0: 1, 1: 2, 3: 1, 4: 1}.get(n, 0)
        if norms:
            @blk.gpsimd
            def _(pool):
                def slot(t, p):
                    if isinstance(t, int) and t >= BLOCKS:
                        return
                    for j in range(norms):
                        st["variance"].wait(pool, norms * t + j + 1)
                        nc.gpsimd.tensor_tensor(small[:, 9:10], small[:, 8:9], sb["minus_half"][:, :],
                                                ALU.pow).then_inc(st["inv_std"].sem, 1)

                slots(slot, pool)

        @blk.scalar
        def _(act):
            uses_exp = n in (1, 2, 5, 6)
            ew = {1: DIM, 2: 512, 5: 2 * prev.heads, 6: 2 * prev.heads}[n] if uses_exp else 0

            def slot(t, p):
                final = isinstance(t, int) and t >= BLOCKS
                if not final:
                    if uses_exp:
                        st["exp_in"].wait(act, t + 1)
                        nc.scalar.activation(e[:, 0:ew], e[:, 0:ew], ACT.Exp).then_inc(st["exp_out"].sem, 1)
                    if L:
                        st["proj_ps"].wait(act, t - 1)
                        st["hT_ps"].wait(act, t + 1)
                        nc.scalar.activation(hT[:, p, 0:L.k], psum_t[p][:, 0:L.k], ACT.Copy).then_inc(
                            st["hT_sb"].sem, 1)
                if L and not (isinstance(t, int) and t == 0):
                    u, q = t - 1, 1 - p
                    k = 16 * (2 if L.extra else 1)
                    if isinstance(u, int):
                        st[f"tb{q}"].wait(act, k * (u // 2))
                    else:
                        st[f"tb{q}"].wait(act, (k // 2) * (u - q))
                    st["proj_ps"].wait(act, u + 1)
                    F, H = L.feat, L.heads
                    nc.scalar.activation(tb[:, q, 0:L.row], psum_f[q][:, 0:L.row], ACT.Copy)
                    if L.extra:
                        nc.scalar.activation(tb[:, q, L.row:], psum_f[q][:, 512:512 + L.extra], ACT.Copy)
                    nc.scalar.activation(sb["er"][:, bass.ds(u * H, H)], psum_f[q][:, F + H:F + 2 * H],
                                         ACT.Copy).then_inc(st["table_sb"].sem, 1)

            if L or uses_exp:
                slots(slot, act)

        if L:
            @blk.tensor
            def _(pe):
                st["w_ready"].wait(pe, 1)

                def slot(t, p):
                    if not (isinstance(t, int) and t >= BLOCKS):
                        st["hT_sb"].wait(pe, t - 1)
                        st["pre_done"].wait(pe, t + 1)
                        for k in range(L.chunks):
                            mm = nc.tensor.transpose(psum_t[p][:, k * P:(k + 1) * P], h[:, p, k * P:(k + 1) * P],
                                                     sb["ident"][:, :])
                        mm.then_inc(st["hT_ps"].sem, 1)
                    if not (isinstance(t, int) and t == 0):
                        u, q = t - 1, 1 - p
                        st["table_sb"].wait(pe, u - 1)
                        st["hT_sb"].wait(pe, u + 1)
                        for lo, hi, at in ((0, split, 0), (split, L.proj, 512)):
                            for k in range(L.chunks):
                                if lo < hi:
                                    mm = nc.tensor.matmul(psum_f[q][:, at:at + hi - lo], hT[:, q, k * P:(k + 1) * P],
                                                          wx[:, k, lo:hi], start=(k == 0), stop=(k == L.chunks - 1))
                        mm.then_inc(st["proj_ps"].sem, 1)

                slots(slot, pe)

    even = (BLOCKS + 1) // 2
    if L:
        for name in ("hT_ps", "hT_sb", "proj_ps", "table_sb"):
            st[name].base += BLOCKS
        st["w_ready"].base += 1
        for p in range(2):
            st[f"tb{p}"].base += 16 * (2 if L.extra else 1) * (even - p)
    st["variance"].base += norms * BLOCKS
    st["inv_std"].base += norms * BLOCKS
    st["w_in"].base += 16 * sb["n_w"]
    st["pre_done"].base += BLOCKS
    if n in (1, 2, 5, 6):
        st["exp_in"].base += BLOCKS
        st["exp_out"].base += BLOCKS
    for p in range(2):
        st[f"in{p}"].base += 16 * len(loads) * (even - p)
        st[f"out{p}"].base += 16 * len(stores) * (even - p)


def edge_pass(nc, st, io, sb, n):
    L = LAYERS[n]
    H, D, F = L.heads, L.depth, L.feat
    CW = L.acc
    HALF = CW // 2 if CW > 512 else CW
    GE = GROUP * P
    act_weighs = H == 1
    with ExitStack() as c:
        def tmp(name, shape, dt=F32):
            return c.enter_context(nc.sbuf_tensor(f"e{n}_{name}", shape, dt))

        rows = [tmp(f"rows{p}", [P, GROUP, CW]) for p in range(2)]
        idx = tmp("idx", [P, 2, GROUP], I32)
        bytes_in = tmp("bytes_in", [P, 2, GE], U8)
        onehot = tmp("onehot", [P, 2, GROUP, P])
        onehot_T = tmp("onehot_T", [P, GROUP, P], BF16)
        er_parts = tmp("er_parts", [P, BLOCKS * H, 3], BF16)
        er_rest = tmp("er_rest", [P, BLOCKS * H])
        er_edge = tmp("er_edge", [P, 2, GROUP, H])
        el = tmp("el", [P, GROUP, H])
        pens = tmp("pens", [MAX_HEADS, 2, 2, GE], BF16)
        forward = tmp("forward", [MAX_HEADS, GE])
        top = tmp("top", [MAX_HEADS, GE + P])
        logit = tmp("logit", [P, 2 * GROUP + 1, H])
        diff = tmp("diff", [P, GROUP, H])
        drop = tmp("drop", [P, H])
        rho = tmp("rho", [P, H])
        ps_el = c.enter_context(nc.psum_tensor(f"e{n}_ps_el", [P, GE], F32))
        ps_sum = [c.enter_context(nc.psum_tensor(f"e{n}_ps_sum{p}", [P, 1024], F32)) for p in range(2)]
        ps_er_all = c.enter_context(nc.psum_tensor(f"e{n}_ps_er", [P, 512], F32))
        ps_small = c.enter_context(nc.psum_tensor(f"e{n}_ps_small", [P, 512], F32))
        ps_er = ps_er_all[:, 0:GROUP * 3 * H].rearrange("p (s h c) -> p s h c", h=H, c=3)
        ps_top = ps_small[:, 0:(GROUP + 1) * H].rearrange("p (s h) -> p s h", h=H)
        ps_rho = ps_small[:, 256:256 + H]
        blk = c.enter_context(nc.Block())

        def slots(fn, eng):
            looped(fn, eng, GROUPS)
            fn(GROUPS, GROUPS % 2)

        def is_last(g):
            return isinstance(g, int) and g >= GROUPS

        def is_first(g):
            return isinstance(g, int) and g == 0

        def blocks_of(kind, g):
            _, got = nc.values_load_multi_w_load_instructions(
                sb["block_of"][0:1, bass.ds(g * GROUP_UNITS, GROUP_UNITS)], engines=(kind,), min_val=0,
                max_val=BLOCKS - 1, skip_runtime_bounds_check_because="the walk's blocks are clamped")
            return got

        @blk.sync
        def _(sp):
            def slot(g, p):
                if is_last(g):
                    return
                st["scanned"].wait(sp, g - 1)
                src = io["pen"][:, bass.ds(g * GE, GE)].unsqueeze(0).to_broadcast([H, 2, GE])
                sp.dma_start(pens[0:H, p, :, :], src).then_inc(st[f"pens{p}"].sem, 16)
                st["onehot"].wait(sp, g - 1)
                sp.dma_start(bytes_in[:, p, :], io["onehot"][bass.ds(g * P, P), :]).then_inc(
                    st[f"bytes{p}"].sem, 16)

            slots(slot, sp)

        @blk.gpsimd
        def _(pool):
            def slot(g, p):
                if is_last(g):
                    return
                st["idx_ready"].wait(pool, g + 1)
                st["summed"].wait(pool, GROUP_UNITS * (g - 1))
                pool.sem_inc(st["gathering"].sem, 1)
                for s in range(GROUP):
                    nc.gpsimd.indirect_dma_start(
                        out=rows[p][:, s, 0:L.row], out_offset=None, in_=io[f"rows{n}"][:, :],
                        in_offset=bass.IndirectOffsetOnAxis(ap=idx[:, p, s:s + 1], axis=0)).then_inc(
                            st[f"rows{p}"].sem, 16)

            slots(slot, pool)

        @blk.vector
        def _(dve):
            v = nc.vector

            def indices(g, p):
                v.tensor_copy(idx[:, p, :], sb["src_of"][:, bass.ds(g * GROUP, GROUP)]).then_inc(
                    st["idx_ready"].sem, 1)

            def split_er():
                for part in range(3):
                    src = sb["er"][:, 0:BLOCKS * H] if part == 0 else er_rest[:, :]
                    v.tensor_copy(er_parts[:, :, part], src)
                    v.drain()
                    if part < 2:
                        v.tensor_tensor(er_rest[:, :], src, er_parts[:, :, part], ALU.subtract)
                        v.drain()
                v.drain().then_inc(st["er_parts"].sem, 1)

            def source_logits(g, p):
                st[f"rows{p}"].wait(dve, 8 * GROUP * (g - p) + 16 * GROUP)
                r = rows[p][:, :, F:F + H]
                if L.edge_term:
                    v.tensor_tensor(el[:, :, 0], rows[p][:, :, F], sb["edge_term"][:, bass.ds(g * GROUP, GROUP)],
                                    ALU.add).then_inc(st["el"].sem, 1)
                else:
                    v.tensor_copy(el[:, :, :], r).then_inc(st["el"].sem, 1)

            def destination_logits(g, p):
                st["er_ps"].wait(dve, g + 1)
                v.tensor_reduce(er_edge[:, p, :, :], ps_er, AX_X, ALU.add).then_inc(st["er_sb"].sem, 1)

            def scans(g, p):
                st[f"pens{p}"].wait(dve, 8 * (g - p) + 16)
                st["el_ps"].wait(dve, g + 1)
                v.tensor_tensor_scan(forward[0:H, :], pens[0:H, p, 0, :], ps_el[0:H, :], sb["carry"][0:H, 0:1],
                                     ALU.add, ALU.max)
                v.tensor_scalar(top[0:H, GE:GE + P], sb["ones"][0:H, :], sb["carry"][0:H, 0:1], None, ALU.mult)
                v.drain()
                v.tensor_tensor_scan(top[0:H, GE - 1::-1], pens[0:H, p, 1, ::-1], forward[0:H, ::-1], LOW,
                                     ALU.add, ALU.max)
                v.tensor_copy(sb["carry"][0:H, 0:1], forward[0:H, GE - 1:GE]).then_inc(st["scanned"].sem, 1)

            def exponents(g, p):
                st["top_ps"].wait(dve, g + 1)
                v.tensor_tensor(logit[:, GROUP:2 * GROUP, :], ps_top[:, 0:GROUP, :], er_edge[:, p, :, :], ALU.add)
                v.tensor_tensor(logit[:, 2 * GROUP, :], ps_top[:, GROUP, :], er_edge[:, p, 0, :], ALU.add)
                v.tensor_tensor(logit[:, 0:GROUP, :], el[:, :, :], er_edge[:, p, :, :], ALU.add)
                if L.self_loop:
                    v.tensor_tensor(rows[p][:, :, F + H:F + 2 * H], ps_top[:, 0:GROUP, :],
                                    sb["ends_here"][:, bass.ds(g * GROUP, GROUP)].unsqueeze(2).to_broadcast(
                                        [P, GROUP, H]), ALU.mult)
                v.drain()
                v.scalar_tensor_tensor(logit[:, :, :], logit[:, :, :], L.slope, logit[:, :, :], ALU.mult, ALU.max)
                v.drain()
                v.tensor_tensor(diff[:, :, :], logit[:, 0:GROUP, :], logit[:, GROUP:2 * GROUP, :], ALU.subtract)
                v.tensor_tensor(drop[:, :], logit[:, 2 * GROUP, :], logit[:, GROUP, :], ALU.subtract)
                v.drain()
                v.tensor_scalar(drop[:, :], drop[:, :], sb["goes_on"][:, bass.ds(g, 1)], None, ALU.mult).then_inc(
                    st["exponents"].sem, 1)

            def message(g, p, s):
                R = rows[p]
                if s == 0:
                    st["weights"].wait(dve, g + 1)
                v.tensor_tensor(per_head(R[:, s, 0:F], H), per_head(R[:, s, 0:F], H),
                                R[:, s, F:F + H].unsqueeze(2).to_broadcast([P, H, D]), ALU.mult).then_inc(
                                    st["message"].sem, 1)

            def rescale(g, blocks):
                st["rho"].wait(dve, g + 1)
                A = sb["acc"][:, bass.ds(blocks[0] * CW, CW)]
                v.tensor_tensor(per_head(A[:, 0:F], H), per_head(A[:, 0:F], H),
                                rho[:, :].unsqueeze(2).to_broadcast([P, H, D]), ALU.mult)
                v.tensor_tensor(A[:, F:F + H], A[:, F:F + H], rho[:, :], ALU.mult)
                v.drain()

            def add(g, k, blocks):
                st["added"].wait(dve, GROUP_UNITS * g + k)
                st["summed"].wait(dve, GROUP_UNITS * g + k + 1)
                A = sb["acc"][:, bass.ds(blocks[k] * CW, CW)].rearrange("p (j c) -> p j c", c=HALF)
                S = ps_sum[k % 2][:, :].rearrange("p (j c) -> p j c", c=512)[:, 0:CW // HALF, 0:HALF]
                v.tensor_tensor(A, A, S, ALU.add).then_inc(st["added"].sem, 1)

            def messages(g, p, lo, hi):
                if not act_weighs:
                    for s in range(lo, hi):
                        message(g, p, s)

            def slot(g, p):
                u, q = g - 1, 1 - p
                if is_first(g):
                    split_er()
                    indices(0, 0)
                    indices(1, 1)
                else:
                    blocks = blocks_of(mybir.EngineType.DVE, u)
                    messages(u, q, 0, 2)
                    rescale(u, blocks)
                    messages(u, q, 2, 4)
                    add(u, 0, blocks)
                if not is_last(g):
                    source_logits(g, p)
                    destination_logits(g, p)
                if not is_first(g):
                    messages(u, q, 4, 6)
                    add(u, 1, blocks)
                    messages(u, q, 6, 8)
                if not is_last(g):
                    scans(g, p)
                if not is_first(g):
                    add(u, 2, blocks)
                    add(u, 3, blocks)
                if not is_last(g):
                    exponents(g, p)
                    indices(g + 2, p)

            slots(slot, dve)

        @blk.tensor
        def _(pe):
            ident = sb["ident"]

            def slot(g, p):
                u, q = g - 1, 1 - p
                if not is_last(g):
                    if is_first(g):
                        st["er_parts"].wait(pe, 1)
                    blocks = blocks_of(mybir.EngineType.PE, g)
                    st["er_sb"].wait(pe, g)
                    st["turned_sb"].wait(pe, g + 1)
                    for s in range(GROUP):
                        mm = nc.tensor.matmul(
                            ps_er[:, s, :, :].rearrange("p h c -> p (h c)"), onehot_T[:, s, :],
                            er_parts[:, bass.ds(blocks[s // UNIT] * H, H), :].rearrange("p h c -> p (h c)"),
                            start=True, stop=True)
                    mm.then_inc(st["er_ps"].sem, 1)

                def sums(k):
                    st["added"].wait(pe, GROUP_UNITS * u + k - 1)
                    for j in range(UNIT):
                        s = UNIT * k + j
                        st["message"].wait(pe, GROUP * u + s + 1)
                        for h in range(CW // HALF):
                            mm = nc.tensor.matmul(ps_sum[k % 2][:, 512 * h:512 * h + HALF], onehot[:, q, s, :],
                                                  rows[q][:, s, HALF * h:HALF * (h + 1)],
                                                  start=(j == 0), stop=(j == UNIT - 1))
                    mm.then_inc(st["summed"].sem, 1)

                if not is_first(g):
                    st["onehot"].wait(pe, g)
                    for k in range(2):
                        sums(k)
                if not is_last(g):
                    st["scanned"].wait(pe, g)
                    st["el"].wait(pe, g + 1)
                    for s in range(GROUP):
                        mm = nc.tensor.transpose(ps_el[0:H, s * P:(s + 1) * P], el[:, s, :], ident[:, :])
                    mm.then_inc(st["el_ps"].sem, 1)
                if not is_first(g):
                    for k in range(2, GROUP_UNITS):
                        sums(k)
                if not is_last(g):
                    st["rho"].wait(pe, g)
                    st["scanned"].wait(pe, g + 1)
                    for s in range(GROUP + 1):
                        mm = nc.tensor.matmul(ps_top[:, s, :], top[0:H, s * P:(s + 1) * P], ident[0:H, 0:H],
                                              start=True, stop=True)
                    mm.then_inc(st["top_ps"].sem, 1)
                    st["onehot"].wait(pe, g + 1)
                    st["exponents"].wait(pe, g + 1)
                    nc.tensor.matmul(ps_rho, onehot[:, p, 0, :], drop[:, :], start=True, stop=True).then_inc(
                        st["rho_ps"].sem, 1)

            slots(slot, pe)

        @blk.scalar
        def _(act):
            def slot(g, p):
                u, q = g - 1, 1 - p
                if not is_last(g):
                    st["er_ps"].wait(act, g)
                    nc.scalar.activation(onehot_T[:, :, :].rearrange("p s e -> p (s e)"),
                                         sb["onehot_T"][:, bass.ds(g * GE, GE)], ACT.Copy).then_inc(
                                             st["turned_sb"].sem, 1)
                if not is_first(g) and act_weighs:
                    R = rows[q]
                    for s in range(GROUP):
                        if s == 0:
                            st["weights"].wait(act, g)
                        nc.scalar.activation(R[:, s, 0:F], R[:, s, 0:F], ACT.Copy,
                                             scale=R[:, s, F:F + 1]).then_inc(st["message"].sem, 1)
                if not is_last(g):
                    st["summed"].wait(act, GROUP_UNITS * (g - 1))
                    st[f"bytes{p}"].wait(act, 8 * (g - p) + 16)
                    nc.scalar.activation(onehot[:, p, :, :].rearrange("p s d -> p (s d)"), bytes_in[:, p, :],
                                         ACT.Copy).then_inc(st["onehot"].sem, 1)
                    st["exponents"].wait(act, g + 1)
                    nc.scalar.activation(rows[p][:, :, F:F + H], diff[:, :, :], ACT.Exp).then_inc(
                        st["weights"].sem, 1)
                    st["rho_ps"].wait(act, g + 1)
                    nc.scalar.activation(rho[:, :], ps_rho, ACT.Exp).then_inc(st["rho"].sem, 1)

            slots(slot, act)

    for name in ("scanned", "idx_ready", "gathering", "onehot", "el", "el_ps", "er_ps", "er_sb", "top_ps",
                 "exponents", "weights", "rho", "rho_ps", "turned_sb"):
        st[name].base += GROUPS
    st["idx_ready"].base += 2
    st["er_parts"].base += 1
    for name in ("summed", "added"):
        st[name].base += GROUPS * GROUP_UNITS
    st["message"].base += GROUPS * GROUP
    for p in range(2):
        st[f"pens{p}"].base += 16 * ((GROUPS + 1 - p) // 2)
        st[f"bytes{p}"].base += 16 * ((GROUPS + 1 - p) // 2)
        st[f"rows{p}"].base += 16 * GROUP * ((GROUPS + 1 - p) // 2)


STAGES = ["variance", "inv_std", "w_in", "w_ready", "pre_done", "exp_in", "exp_out", "hT_ps", "hT_sb", "proj_ps", "table_sb",
          "in0", "in1", "out0", "out1", "tb0", "tb1",
          "scanned", "idx_ready", "gathering", "onehot", "el", "el_ps", "er_ps", "er_sb", "top_ps", "exponents",
          "weights", "rho", "rho_ps", "turned_sb", "er_parts", "oh_used", "oh_in0", "oh_in1", "oh_out0", "oh_out1", "bytes0", "bytes1", "message", "summed", "added",
          "pens0", "pens1", "rows0", "rows1"]


def build(nc, io):
    with ExitStack() as ctx:
        def keep(name, shape, dt=F32):
            return ctx.enter_context(nc.sbuf_tensor(name, shape, dt))

        sb = {
            "acc": keep("acc", [P, BLOCKS * MAX_ACC]),
            "er": keep("er", [P, BLOCKS * MAX_HEADS]),
            "src_of": keep("src_of", [P, STEPS + 2 * GROUP], I32),
            "dst_in_block": keep("dst_in_block", [P, STEPS]),
            "ends_here": keep("ends_here", [P, STEPS]),
            "edge_term": keep("edge_term", [P, STEPS]),
            "goes_on": keep("goes_on", [P, GROUPS]),
            "block_of": keep("block_of", [P, WALK], I32),
            "onehot_T": keep("onehot_nodes", [P, STEPS * P], U8),
            "lane": keep("lane", [P, 1]),
            "ident": keep("ident", [P, P]),
            "iota": keep("iota", [P, P]),
            "ones": keep("ones", [P, P]),
            "carry": keep("carry", [P, 1]),
            "minus_half": keep("minus_half", [P, 1]),
        }
        st = {name: Stage(nc, ctx, name) for name in STAGES}

        def scratch(name, shape, dt=F32):
            return nc.dram_tensor("dram_" + name, shape, dt, kind="Internal").ap()

        NP = BLOCKS * P
        io["walk_rows"] = scratch("walk_rows", [WALK_ROWS * P * UE + 2 * P], I32)
        io["walk_block"] = scratch("walk_block", [WALK_ROWS * P], I32)
        io["ea_flat"] = scratch("ea_flat", [P, UNITS * UNIT])
        io["ea_units"] = io["ea_flat"].rearrange("p j -> (p j)").rearrange("(t q) -> t q", q=UE)
        io["dst_local"] = scratch("dst_local", [WALK_ROWS * P * UE], BF16)
        io["pen"] = scratch("pen", [2, WALK_ROWS * P * UE], BF16)
        io["onehot"] = scratch("onehot", [GROUPS * P, GROUP * P], U8)
        io["x_mid"] = scratch("x_mid", [NP, DIM])
        io["h_mid"] = scratch("h_mid", [NP, DIM])
        io["hs_mid"] = scratch("hs_mid", [NP, DIM])
        for n, L in enumerate(LAYERS):
            io[f"rows{n}"] = scratch(f"rows_table{n}", [NP, L.row])

        with nc.Block() as blk:
            @blk.vector
            def _(dve):
                nc.vector.memset(sb["ones"][:, :], 1.0)
                nc.vector.memset(sb["minus_half"][:, :], -0.5)
                nc.vector.memset(sb["src_of"][:, STEPS:], 0)
        prepare(nc, ctx, st, io, {**sb, "src_of": sb["src_of"][:, 0:STEPS]})
        make_onehots(nc, st, io, sb)
        for n in range(len(LAYERS) + 1):
            node_phase(nc, st, io, sb, n)
            if n < len(LAYERS):
                edge_pass(nc, st, io, sb, n)


def kernel(**inputs):
    import numpy as np
    import concourse.bacc as bacc
    from concourse import mybir as mb
    from concourse.bass_utils import run_bass_kernel_spmd as run

    x = {k: np.asarray(v) for k, v in inputs.items()}
    NP, EP = BLOCKS * P, UNITS * UE

    def pad(a, rows, fill):
        out = np.full((rows,) + a.shape[1:], fill, a.dtype)
        out[:a.shape[0]] = a
        return out

    dst = pad(x["dst"], EP, NO_NODE)
    arrays = {
        "x": pad(x["x"], NP, 0),
        "src_units": pad(x["src"], EP, 0).reshape(UNITS, UE),
        "dst_units": dst.reshape(UNITS, UE),
        "dst_last": dst.reshape(UNITS, UE)[:UNITS - 1, UE - 1],
        "edge_attr": pad(x["edge_attr_64"], EP, 0).reshape(P, UNITS * UNIT * EDGE_DIM),
        "iota": np.arange(512, dtype=np.float32),
        "step_no": np.arange(WALK_ROWS * P, dtype=np.float32).reshape(WALK_ROWS, P).T,
        "ident": np.eye(P, dtype=np.float32),
        "lane": np.arange(P, dtype=np.float32).reshape(P, 1),
        "no_node": np.full((P,), -1, np.int32),
        "att": x["L2_gnn_W_att"].reshape(-1),
        "gamma": x["L0_gnn_gamma"], "beta": x["L0_gnn_beta"],
        "b1": x["L3_gnn_b1"], "b2": x["L3_gnn_b2"], "prelu": x["L3_gnn_prelu_w"].reshape(1),
        "w0": x["L0_gnn_W"], "w1": x["L1_gnn_W1"], "w2": x["L1_gnn_W2"],
        "w3": np.concatenate([x["L2_gnn_W_func"].T, x["L2_gnn_W_self"].T], axis=1),
        "w4": x["L3_gnn_W1"], "w5": x["L3_gnn_W2"],
        "a0": np.stack([x["L0_gnn_a_src"].reshape(-1), x["L0_gnn_a_dst"].reshape(-1)]),
        "a1": np.stack([x["L1_gnn_attn_l1"].reshape(-1), x["L1_gnn_attn_r1"].reshape(-1)]),
        "a2": np.stack([x["L1_gnn_attn_l2"].reshape(-1), x["L1_gnn_attn_r2"].reshape(-1)]),
        "a3": x["L2_gnn_W_att"].reshape(-1)[:2 * DIM].reshape(2, DIM),
        "a4": np.stack([x["L3_gnn_a_src1"].reshape(-1), x["L3_gnn_a_dst1"].reshape(-1)]),
        "a5": np.stack([x["L3_gnn_a_src2"].reshape(-1), x["L3_gnn_a_dst2"].reshape(-1)]),
    }
    arrays = {"in_" + k: np.ascontiguousarray(v) for k, v in arrays.items()}
    nc = bacc.Bacc("TRN2", target_bir_lowering=False, num_devices=1)
    io = {k[3:]: nc.dram_tensor(k, v.shape, mb.dt.from_np(v.dtype), kind="ExternalInput").ap() for k, v in arrays.items()}
    io["out"] = nc.dram_tensor("out", (NP, DIM), mb.dt.float32, kind="ExternalOutput").ap()
    build(nc, io)
    r = run(nc, [arrays], core_ids=[0])
    return r.results[0]["out"][:NODES]
```

```python
from contextlib import ExitStack

import concourse.bass as bass
import concourse.mybir as mybir

F32 = mybir.dt.float32
BF16 = mybir.dt.bfloat16
I32 = mybir.dt.int32
U8 = mybir.dt.uint8
ALU = mybir.AluOpType
ACT = mybir.ActivationFunctionType
AX_X = mybir.AxisListType.X

P = 128
NODES = 3125
EDGES = 50000
DIM = 256
EDGE_DIM = 64
BLOCKS = -(-NODES // P)
TILES = -(-EDGES // P)
UNIT = 2
UNITS = -(-TILES // UNIT)
UE = UNIT * P
GROUP_UNITS = 4
GROUP = GROUP_UNITS * UNIT
GROUPS = -(-(UNITS + BLOCKS - 1) // GROUP_UNITS)
WALK = GROUPS * GROUP_UNITS
STEPS = GROUPS * GROUP
WALK_ROWS = -(-WALK // P)
NO_NODE = 4095
LN_EPS = 1e-5
LOW = -1e30
TINY = 1e-30
MAX_HEADS = 8
MAX_ACC = 528


class Stage:

    def __init__(self, nc, ctx, name):
        self.sem = ctx.enter_context(nc.semaphore(name))
        self.base = 0

    def at(self, count):
        if isinstance(count, int):
            return self.sem, max(self.base + count, 0)
        return self.sem, self.base + count


class Layer:

    def __init__(self, heads, depth, k, slope, self_loop=False, edge_term=False, extra=0):
        self.heads, self.depth, self.k, self.slope = heads, depth, k, slope
        self.self_loop, self.edge_term, self.extra = self_loop, edge_term, extra
        self.feat = heads * depth
        self.row = self.feat + heads
        self.acc = self.feat + (2 if self_loop else 1) * heads
        self.proj = self.feat + 2 * heads + extra
        self.chunks = k // P


LAYERS = [
    Layer(8, 32, 256, 0.2),
    Layer(8, 64, 256, 0.2),
    Layer(1, 256, 512, 0.2),
    Layer(1, 256, 256, 0.01, edge_term=True, extra=256),
    Layer(4, 128, 256, 0.2, self_loop=True),
    Layer(1, 256, 512, 0.2, self_loop=True),
]


def per_head(ap, heads):
    return ap.rearrange("p (h d) -> p h d", h=heads)


def looped(fn, eng, count):
    fn(0, 0, 0)
    fn(1, 1, 0)
    with eng.Fori(0, (count - 2) // 2) as i:
        for p in range(2):
            fn(2 * i + 2 + p, p, i + 1)
    if count % 2:
        fn(count - 1, 0, count // 2)


ACT_STEPS = [[1, 3, 4, 6], [1, 3, 4, 6], list(range(GROUP)), list(range(GROUP)), [1, 2, 3, 4, 6, 7],
             list(range(GROUP))]
MAX_RING = 4


class Slot:

    def __init__(self, ring, first, i=0):
        period = ring if ring % 2 == 0 else 2 * ring
        self.first, self.ring = first, ring
        self.known = isinstance(i, int)
        self.no = first + period * i
        self.p, self.r = first % 2, first % ring
        self.half = first // 2 + (period // 2) * i
        self.period_turns = (period // ring) * i

    def turn(self, ahead=0):
        return (self.first + ahead) // self.ring + self.period_turns

    def at_least(self, count):
        return self.first >= count

    def within(self, ahead):
        return not self.known or self.no + ahead < GROUPS


def slots_of_pass(fn, eng, ring):
    period = ring if ring % 2 == 0 else 2 * ring
    rounds = (GROUPS - 2 - ring) // period
    for first in range(ring):
        fn(Slot(ring, first))
    with eng.Fori(0, rounds) as i:
        for j in range(period):
            fn(Slot(ring, ring + j, i))
    for first in range(ring + rounds * period, GROUPS + 1):
        fn(Slot(ring, first))


def prepare(nc, ctx, st, io, sb):
    row_of = io["walk_rows"]
    W = WALK_ROWS * P * UE
    with ExitStack() as c:
        def tmp(name, shape, dt=F32):
            return c.enter_context(nc.sbuf_tensor(name, shape, dt))

        def sem(name):
            return c.enter_context(nc.semaphore(name))

        last = tmp("last_dst", [P, UNITS - 1], I32)
        leave = tmp("leave_step", [P, UNITS - 1])
        iota_units = tmp("iota_units", [P, UNITS - 1])
        passed = tmp("passed", [P, UNITS - 1])
        step_no = tmp("step_no", [P, WALK_ROWS])
        unit_f = tmp("unit_f", [P, WALK_ROWS])
        unit_i = tmp("unit_i", [P, WALK_ROWS], I32)
        block_f = tmp("block_f", [P, WALK_ROWS])
        block_i = tmp("block_i", [P, WALK_ROWS], I32)
        src_rows = tmp("src_rows", [P, WALK_ROWS, UE], I32)
        dst_rows = tmp("dst_rows", [P, WALK_ROWS, UE], I32)
        dst_before = tmp("dst_before", [P, WALK_ROWS, UE], I32)
        dst_after = tmp("dst_after", [P, WALK_ROWS, UE], I32)
        ea_rows = tmp("ea_rows", [P, WALK_ROWS, UE])
        src_f = tmp("src_f", [P, WALK_ROWS, UE])
        dst_f = tmp("dst_f", [P, WALK_ROWS, UE])
        dst_bf = tmp("dst_bf", [P, WALK_ROWS, UE], BF16)
        starts = tmp("starts", [P, WALK_ROWS, UE])
        ends = tmp("ends", [P, WALK_ROWS, UE])
        pen = tmp("pen", [P, 2, WALK_ROWS, UE], BF16)
        goes = tmp("goes", [P, GROUPS])
        att_e = tmp("att_e", [P, EDGE_DIM])
        EPP = UNITS * UNIT
        NCH = 4
        CH = -(-EPP // NCH)
        ea_in = tmp("ea_in", [P, 2, CH * EDGE_DIM])
        ea_out = tmp("ea_out", [P, EPP])
        psum = [c.enter_context(nc.psum_tensor(f"turn{k}", [P, 512], F32)) for k in range(5)]

        s_in, s_att, s_t, s_b, s_ea_st, s_seq, s_sh, s_bi = (sem(n) for n in (
            "prep_in", "att_in", "unit_index", "block_store", "ea_store", "walk_dst_store", "shifted", "block_row"))
        s_eain = [sem("ea_in0"), sem("ea_in1")]
        s_g = [sem("src_got"), sem("dst_got"), sem("ea_got")]
        s_eadone, s_walk, s_mark, s_pen, s_turned, s_dve = (sem(n) for n in (
            "ea_chunk_done", "walk_f_ready", "marks_ready", "pen_store", "tables_turned", "prep_done"))
        blk = c.enter_context(nc.Block())

        @blk.sync
        def _(sp):
            sp.dma_start(last[:, :], io["dst_last"].partition_broadcast(P)).then_inc(s_in, 16)
            sp.dma_start(iota_units[:, :], io["iota"][0:UNITS - 1].partition_broadcast(P)).then_inc(s_in, 16)
            sp.dma_start(step_no[:, :], io["step_no"][:, :]).then_inc(s_in, 16)
            sp.dma_start(sb["ident"][:, :], io["ident"][:, :]).then_inc(s_in, 16)
            sp.dma_start(sb["iota"][:, :], io["iota"][0:P].partition_broadcast(P)).then_inc(s_in, 16)
            sp.dma_start(sb["lane"][:, :], io["lane"][:, :]).then_inc(s_in, 16)
            sp.dma_start(att_e[:, :], io["att"][2 * DIM:2 * DIM + EDGE_DIM].partition_broadcast(P)).then_inc(s_att, 16)
            for n in range(NCH):
                w = min(CH, EPP - n * CH)
                if n >= 2:
                    sp.wait_ge(s_eadone, n - 1)
                sp.dma_start(ea_in[:, n % 2, 0:w * EDGE_DIM],
                             io["edge_attr"][:, n * CH * EDGE_DIM:(n * CH + w) * EDGE_DIM]).then_inc(s_eain[n % 2], 16)
            sp.wait_ge(s_eadone, NCH)
            sp.dma_start(io["ea_flat"][:, :], ea_out[:, :]).then_inc(s_ea_st, 16)

        @blk.scalar
        def _(act):
            act.wait_ge(s_t, 2)
            with nc.allow_non_contiguous_dma(reason="one number per unit"):
                act.dma_start(io["walk_block"].rearrange("(k p) -> p k", p=P), block_i[:, :]).then_inc(s_b, 16)
            act.wait_ge(s_b, 16)
            act.dma_start(sb["block_of"][0:1, :], io["walk_block"][0:WALK].unsqueeze(0)).then_inc(s_bi, 16)
            act.wait_ge(s_g[1], 16 * WALK_ROWS)
            seq = row_of[P:P + W].rearrange("(k p q) -> p k q", p=P, q=UE)
            act.dma_start(seq, dst_rows[:, :, :]).then_inc(s_seq, 16)
            act.dma_start(row_of[0:P].unsqueeze(0), io["no_node"].unsqueeze(0)).then_inc(s_seq, 16)
            act.dma_start(row_of[P + W:2 * P + W].unsqueeze(0), io["no_node"].unsqueeze(0)).then_inc(s_seq, 16)
            act.wait_ge(s_seq, 48)
            for buf, off in ((dst_before, P - 1), (dst_after, P + 1)):
                view = row_of[off:off + W].rearrange("(k p q) -> p k q", p=P, q=UE)
                act.dma_start(buf[:, :, :], view).then_inc(s_sh, 16)
            act.wait_ge(s_walk, 1)
            act.dma_start(io["dst_local"].rearrange("(k p q) -> p k q", p=P, q=UE), dst_bf[:, :, :]).then_inc(s_pen, 16)
            act.wait_ge(s_mark, 1)
            for d in range(2):
                view = io["pen"][d].rearrange("(k p q) -> p k q", p=P, q=UE)
                act.dma_start(view, pen[:, d, :, :]).then_inc(s_pen, 16)
            act.wait_ge(s_pen, 48)
            act.wait_ge(s_bi, 16)

        @blk.gpsimd
        def _(pool):
            pool.wait_ge(s_t, 1)
            for k in range(WALK_ROWS):
                for buf, table, s in ((src_rows, "src_units", s_g[0]), (dst_rows, "dst_units", s_g[1])):
                    nc.gpsimd.indirect_dma_start(
                        out=buf[:, k, :], out_offset=None, in_=io[table][:, :],
                        in_offset=bass.IndirectOffsetOnAxis(ap=unit_i[:, k:k + 1], axis=0)).then_inc(s, 16)
            pool.wait_ge(s_ea_st, 16)
            for k in range(WALK_ROWS):
                nc.gpsimd.indirect_dma_start(
                    out=ea_rows[:, k, :], out_offset=None, in_=io["ea_units"][:, :],
                    in_offset=bass.IndirectOffsetOnAxis(ap=unit_i[:, k:k + 1], axis=0)).then_inc(s_g[2], 16)

        @blk.vector
        def _(dve):
            v = nc.vector
            dve.wait_ge(s_in, 96)
            v.tensor_scalar(last[:, :], last[:, :], 7, None, ALU.arith_shift_right)
            v.drain()
            v.tensor_tensor(leave[:, :], last[:, :], iota_units[:, :], ALU.add)
            v.drain()
            for k in range(WALK_ROWS):
                v.tensor_scalar(passed[:, :], leave[:, :], step_no[:, k:k + 1], None, ALU.is_lt)
                v.drain()
                v.tensor_reduce(unit_f[:, k:k + 1], passed[:, :], AX_X, ALU.add)
                v.drain()
            v.tensor_copy(unit_i[:, :], unit_f[:, :]).then_inc(s_t, 1)
            v.tensor_tensor(block_f[:, :], step_no[:, :], unit_f[:, :], ALU.subtract)
            v.drain()
            v.tensor_scalar(block_i[:, :], block_f[:, :], float(BLOCKS - 1), None, ALU.min).then_inc(s_t, 1)
            v.tensor_scalar(block_f[:, :], block_f[:, :], float(P), None, ALU.mult)
            dve.wait_ge(s_att, 16)
            for n in range(NCH):
                w = min(CH, EPP - n * CH)
                dve.wait_ge(s_eain[n % 2], 16 * (n // 2 + 1))
                view = ea_in[:, n % 2, 0:w * EDGE_DIM].rearrange("p (j d) -> p j d", d=EDGE_DIM)
                v.tensor_tensor(view, view, att_e[:, :].unsqueeze(1).to_broadcast([P, w, EDGE_DIM]), ALU.mult)
                v.drain()
                v.tensor_reduce(ea_out[:, n * CH:n * CH + w], view, AX_X, ALU.add).then_inc(s_eadone, 1)
            dve.wait_ge(s_g[0], 16 * WALK_ROWS)
            dve.wait_ge(s_g[1], 16 * WALK_ROWS)
            v.tensor_copy(src_f[:, :, :], src_rows[:, :, :])
            for k in range(WALK_ROWS):
                v.tensor_scalar(dst_f[:, k, :], dst_rows[:, k, :], block_f[:, k:k + 1], None, ALU.subtract)
                v.tensor_scalar(dst_bf[:, k, :], dst_rows[:, k, :], block_f[:, k:k + 1], None, ALU.subtract)
            v.drain().then_inc(s_walk, 1)
            dve.wait_ge(s_sh, 32)
            v.tensor_tensor(starts[:, :, :], dst_rows[:, :, :], dst_before[:, :, :], ALU.not_equal)
            v.tensor_tensor(ends[:, :, :], dst_rows[:, :, :], dst_after[:, :, :], ALU.not_equal)
            v.drain()
            v.tensor_scalar(pen[:, 0, :, :], starts[:, :, :], LOW, None, ALU.mult)
            v.tensor_scalar(pen[:, 1, :, :], ends[:, :, :], LOW, None, ALU.mult)
            v.drain().then_inc(s_mark, 1)
            for n, dst in enumerate((sb["src_of"], sb["dst_in_block"], sb["ends_here"], None, sb["edge_term"])):
                dve.wait_ge(s_turned, n + 1)
                by_half = psum[n][:, :].rearrange("p (j u) -> p j u", j=UNIT)
                if dst is None:
                    v.tensor_copy(goes[:, :], by_half[:, 0, 0:WALK:GROUP_UNITS])
                else:
                    for j in range(UNIT):
                        v.tensor_copy(dst[:, j:STEPS:UNIT], by_half[:, j, 0:WALK])
            v.drain()
            v.tensor_scalar(goes[:, :], goes[:, :], -1.0, 1.0, ALU.mult, ALU.add)
            v.drain()
            v.tensor_scalar(sb["goes_on"][:, :], goes[:, :], sb["ident"][:, 0:1], None, ALU.mult)
            v.drain().then_inc(s_dve, 1)

        @blk.tensor
        def _(pe):
            pe.wait_ge(s_in, 96)
            for n, rows in enumerate((src_f, dst_f, ends, starts, ea_rows)):
                if n == 0:
                    pe.wait_ge(s_walk, 1)
                if n == 2:
                    pe.wait_ge(s_mark, 1)
                if n == 4:
                    pe.wait_ge(s_g[2], 16 * WALK_ROWS)
                for k in range(WALK_ROWS):
                    for j in range(UNIT):
                        at = (j * WALK_ROWS + k) * P
                        mm = nc.tensor.transpose(psum[n][:, at:at + P], rows[:, k, j * P:(j + 1) * P],
                                                 sb["ident"][:, :])
                mm.then_inc(s_turned, 1)


def make_onehots(nc, st, io, sb):
    GE = GROUP * P
    with ExitStack() as c:
        rows = c.enter_context(nc.sbuf_tensor("dst_bcast", [P, 2, GE], BF16))
        flat = c.enter_context(nc.sbuf_tensor("onehot_bytes", [P, 2, GROUP, P], U8))
        blk = c.enter_context(nc.Block())

        @blk.sync
        def _(sp):
            def slot(g, p, k):
                sp.wait_ge(*st["oh_used"].at(g - 1))
                sp.dma_start(rows[:, p, :], io["dst_local"][bass.ds(g * GE, GE)].partition_broadcast(P)).then_inc(
                    st[f"oh_in{p}"].sem, 16)

            looped(slot, sp, GROUPS)

        @blk.vector
        def _(dve):
            v = nc.vector

            def slot(g, p, k):
                dve.wait_ge(*st[f"oh_out{p}"].at(16 * k))
                v.tensor_tensor(flat[:, p, :, :], sb["iota"][:, :].unsqueeze(1).to_broadcast([P, GROUP, P]),
                                sb["dst_in_block"][:, bass.ds(g * GROUP, GROUP)].unsqueeze(2).to_broadcast(
                                    [P, GROUP, P]), ALU.is_equal).then_inc(st["oh_flat"].sem, 1)
                dve.wait_ge(*st[f"oh_in{p}"].at(16 * (k + 1)))
                v.tensor_scalar(sb["onehot_T"][:, bass.ds(g * GE, GE)], rows[:, p, :], sb["lane"][:, 0:1], None,
                                ALU.is_equal).then_inc(st["oh_used"].sem, 1)

            looped(slot, dve, GROUPS)

        @blk.scalar
        def _(act):
            def slot(g, p, k):
                act.wait_ge(*st["oh_flat"].at(g + 1))
                act.dma_start(io["onehot"][bass.ds(g * P, P), :],
                              flat[:, p, :, :].rearrange("p s d -> p (s d)")).then_inc(st[f"oh_out{p}"].sem, 16)

            looped(slot, act, GROUPS)
            for p in range(2):
                act.wait_ge(*st[f"oh_out{p}"].at(16 * ((GROUPS + 1 - p) // 2)))


NODE_RING = 4
LAST_STAGE = [1, 3, 1, 1, 1, 0, 0]
EXP_STAGE = {1: 1, 2: 0}
NORM_STAGES = {0: [0], 1: [0, 2], 3: [0], 4: [0]}


class Tile:

    def __init__(self, first, i=0):
        self.known = isinstance(i, int)
        self.first = first
        self.no = first + NODE_RING * i
        self.b = first % NODE_RING
        self.turn = first // NODE_RING + i

    @property
    def reused(self):
        return self.first >= NODE_RING


def slots_of_nodes(fn, eng, n):
    last_lag = LAST_STAGE[n] + 3
    first = last_lag + NODE_RING
    rounds = (BLOCKS - 1 - first) // NODE_RING

    def known(s):
        fn(lambda lag: Tile(s - lag) if 0 <= s - lag < BLOCKS else None)

    for s in range(-1, first):
        known(s)
    with eng.Fori(0, rounds) as i:
        for j in range(NODE_RING):
            fn(lambda lag: Tile(first + j - lag, i))
    for s in range(first + rounds * NODE_RING, BLOCKS + last_lag):
        known(s)


def node_phase(nc, st, io, sb, n):
    L = LAYERS[n] if n < len(LAYERS) else None
    prev = LAYERS[n - 1] if n else None
    loads = [["x"], ["x", "h"], [], ["x"], ["x", "h", "hs"], ["table"], ["x", "table"]][n]
    stores = [["h"], ["x"], [], ["x", "h"], ["x"], [], ["out"]][n]
    last = LAST_STAGE[n]
    norms = NORM_STAGES.get(n, [])
    joined = bool(prev and prev.self_loop)
    with ExitStack() as c:
        def tmp(name, shape, dt=F32):
            return c.enter_context(nc.sbuf_tensor(f"n{n}_{name}", shape, dt))

        R = NODE_RING
        width = {"x": DIM, "h": DIM, "hs": DIM, "table": prev.feat if prev else 0}
        tin = {name: tmp("in_" + name, [P, R, width[name]]) for name in loads}
        xo = tmp("x_out", [P, R, DIM])
        h = tmp("h", [P, R, 512])
        a = tmp("a", [P, R, 512])
        b = tmp("b", [P, R, 512])
        e = tmp("e", [P, R, 512])
        small = tmp("small", [P, R, 16])
        vec = tmp("vec", [P, 2, 512])
        vec1 = tmp("vec1", [P, 1])
        ph = prev.heads if prev else 1
        per_node = tmp("per_node", [P, 8, BLOCKS * ph])
        psum_t = [c.enter_context(nc.psum_tensor(f"n{n}_ps_hT{k}", [P, 512], F32)) for k in range(R)]
        psum_f = [c.enter_context(nc.psum_tensor(f"n{n}_ps_proj{k}", [P, 1024], F32)) for k in range(2)]
        if L:
            wx = tmp("wx", [P, L.chunks, L.proj])
            wtmp = tmp("wtmp", [P, 2, L.chunks, L.feat])
            avec = tmp("avec", [P, 2, L.feat])
            hT = tmp("hT", [P, R, 512])
            tb = tmp("tb", [P, R, L.row + L.extra])
        split = min(512, L.proj) if L else 0
        if L and L.extra:
            split = L.feat + 2 * L.heads
        blk = c.enter_context(nc.Block())

        dram = {"x": io["x"] if n <= 1 else io["x_mid"], "h": io["h_mid"], "hs": io["hs_mid"],
                "table": io[f"rows{n - 1}"] if n else None}
        sto = {"x": io["x_mid"], "h": io["h_mid"], "out": io["out"]}
        tb_stores = (2 if L.extra else 1) if L else 0
        w_loads = []
        if L:
            wsrc = io[f"w{n}"]
            for k in range(L.chunks):
                w_loads.append((wx[:, k, 0:L.feat], wsrc[k * P:(k + 1) * P, 0:L.feat]))
                if L.extra:
                    w_loads.append((wx[:, k, L.feat + 2 * L.heads:], wsrc[k * P:(k + 1) * P, L.feat:]))
            for j in range(2):
                w_loads.append((avec[:, j, :], io[f"a{n}"][j].partition_broadcast(P)))
        for j, name in enumerate({1: ["gamma", "beta"], 5: ["b1"], 6: ["b2"]}.get(n, [])):
            wide = 512 if n == 5 else DIM
            w_loads.append((vec[:, j, 0:wide], io[name].partition_broadcast(P)))
        if n == 5:
            w_loads.append((vec1[:, :], io["prelu"].partition_broadcast(P)))

        def rows(t):
            return bass.ds(t.no * P, P)

        @blk.sync
        def _(sp):
            def slot(behind):
                t = behind(-1)
                if t and loads:
                    if t.first >= NODE_RING:
                        sp.wait_ge(*st["pre_done"].at(t.no - NODE_RING + 1))
                    for name in loads:
                        sp.dma_start(tin[name][:, t.b, :], dram[name][rows(t), 0:width[name]]).then_inc(
                            st[f"in{t.b}"].sem, 16)
                t = behind(0)
                if t and t.known and t.no == 0:
                    for dst, src in w_loads:
                        sp.dma_start(dst, src).then_inc(st["w_in"].sem, 16)
                t = behind(last + 1)
                if t and stores:
                    sp.wait_ge(*st["pre_done"].at(t.no + 1))
                    for name in stores:
                        src = {"x": xo, "out": xo, "h": h}[name]
                        sp.dma_start(sto[name][rows(t), 0:DIM], src[:, t.b, 0:DIM]).then_inc(st[f"out{t.b}"].sem, 16)
                t = behind(last + 3)
                if t and L:
                    sp.wait_ge(*st["table_sb"].at(t.no + 1))
                    sp.dma_start(io[f"rows{n}"][rows(t), 0:L.row], tb[:, t.b, 0:L.row]).then_inc(
                        st[f"tb{t.b}"].sem, 16)
                    if L.extra:
                        sp.dma_start(io["hs_mid"][rows(t), :], tb[:, t.b, L.row:]).then_inc(st[f"tb{t.b}"].sem, 16)

            slots_of_nodes(slot, sp, n)
            for k in range(R):
                tiles = (BLOCKS + R - 1 - k) // R
                sp.wait_ge(*st[f"out{k}"].at(16 * tiles * len(stores)))
                sp.wait_ge(*st[f"tb{k}"].at(16 * tiles * tb_stores))

        @blk.vector
        def _(dve):
            v = nc.vector

            def weights():
                dve.wait_ge(*st["w_in"].at(16 * len(w_loads)))
                if L:
                    for k in range(L.chunks):
                        for j in range(2):
                            v.tensor_tensor(wtmp[:, j, k, :], wx[:, k, 0:L.feat], avec[:, j, :], ALU.mult)
                    v.drain()
                    for k in range(L.chunks):
                        for j in range(2):
                            v.tensor_reduce(wx[:, k, L.feat + j * L.heads:L.feat + (j + 1) * L.heads],
                                            per_head(wtmp[:, j, k, :], L.heads), AX_X, ALU.add)
                    v.drain().then_inc(st["w_ready"].sem, 1)

            def moments(src, t, which=0):
                v.bn_stats(small[:, t.b, 0:6], src)
                v.drain()
                v.bn_aggr(small[:, t.b, 6:8], small[:, t.b, 0:6]).then_inc(
                    st[f"variance{which}"].sem, 1)

            def scaled(dst, src, t, which=0):
                dve.wait_ge(*st[f"inv_std{which}"].at(t.no + 1))
                return v.tensor_scalar(dst, src, small[:, t.b, 6:7], small[:, t.b, 9:10], ALU.subtract, ALU.mult)

            def sums(t):
                return sb["acc"][:, bass.ds(t.no * prev.acc, prev.acc)]

            def node(k, t, head=0, heads=1):
                return per_node[:, k, bass.ds(t.no * ph + head, heads)]

            def over_nodes(k):
                return per_node[:, k, :].rearrange("p (t h) -> p t h", h=ph)

            def factors():
                H, F = prev.heads, prev.feat
                A = sb["acc"][:, 0:BLOCKS * prev.acc].rearrange("p (t c) -> p t c", c=prev.acc)
                den = A[:, :, F:F + H]
                if not joined:
                    v.tensor_scalar(over_nodes(1), den, TINY, None, ALU.max)
                    if n == 4:
                        v.tensor_scalar(over_nodes(2), den, 0.5, None, ALU.is_gt)
                        v.tensor_scalar(over_nodes(3), den, 0.5, None, ALU.is_lt)
                    v.drain()
                    v.reciprocal(per_node[:, 0, :], per_node[:, 1, :])
                    v.drain()
                    return
                er, el = sb["er"][:, 0:BLOCKS * H], sb["el_own"][:, 0:BLOCKS * H]
                s = [per_node[:, k, :] for k in range(8)]
                v.tensor_scalar(over_nodes(2), den, 0.5, None, ALU.is_lt)
                v.tensor_tensor(s[4], el, er, ALU.add)
                v.drain()
                v.scalar_tensor_tensor(over_nodes(3), over_nodes(2), LOW, A[:, :, F + H:F + 2 * H], ALU.mult, ALU.add)
                v.drain()
                v.tensor_tensor(s[5], s[3], el, ALU.max)
                v.drain()
                v.tensor_tensor(s[3], s[3], er, ALU.add)
                v.tensor_tensor(s[5], s[5], er, ALU.add)
                v.drain()
                v.scalar_tensor_tensor(per_node[:, 3:6, :], per_node[:, 3:6, :], prev.slope, per_node[:, 3:6, :],
                                       ALU.mult, ALU.max)
                v.drain()
                v.tensor_tensor(s[6], s[3], s[5], ALU.subtract)
                v.tensor_tensor(s[7], s[4], s[5], ALU.subtract)
                v.drain().then_inc(st["exp_in"].sem, 1)
                dve.wait_ge(*st["exp_out"].at(1))
                v.tensor_tensor(over_nodes(2), den, over_nodes(6), ALU.mult)
                v.drain()
                v.tensor_tensor(s[2], s[2], s[7], ALU.add)
                v.drain()
                v.reciprocal(s[3], s[2])
                v.drain()
                v.tensor_tensor(s[0], s[6], s[3], ALU.mult)
                v.tensor_tensor(s[1], s[7], s[3], ALU.mult)
                v.drain()

            def divide(dst, t):
                H, F = prev.heads, prev.feat
                v.tensor_tensor(per_head(dst, H), per_head(sums(t)[:, 0:F], H),
                                node(0, t, 0, H).unsqueeze(2).to_broadcast([P, H, prev.depth]), ALU.mult)
                v.drain()

            def join_self(t):
                H, D = prev.heads, prev.depth
                for k in range(H):
                    at = slice(k * D, (k + 1) * D)
                    v.scalar_tensor_tensor(a[:, t.b, at], sums(t)[:, at], node(0, t, k), vec[:, 0, at],
                                           ALU.mult, ALU.add)
                v.drain()
                for k in range(H):
                    at = slice(k * D, (k + 1) * D)
                    v.scalar_tensor_tensor(a[:, t.b, at], tin["table"][:, t.b, at], node(1, t, k), a[:, t.b, at],
                                           ALU.mult, ALU.add)
                v.drain()

            def begin(t):
                if loads:
                    dve.wait_ge(*st[f"in{t.b}"].at(16 * len(loads) * (t.turn + 1)))

            def outputs_free(t):
                if L:
                    if t.first >= NODE_RING:
                        dve.wait_ge(*st["hT_ps"].at(t.no - NODE_RING + 1))
                if stores:
                    if t.reused:
                        dve.wait_ge(*st[f"out{t.b}"].at(16 * len(stores) * t.turn))

            def stage(j, t):
                k = t.b
                x_in = tin["x"][:, k, :] if "x" in tin else None
                at_, bt, et, xn, hn = a[:, k, 0:DIM], b[:, k, 0:DIM], e[:, k, 0:DIM], xo[:, k, :], h[:, k, 0:DIM]
                if j == 0:
                    begin(t)
                    if not norms or n == 3 or n == 4:
                        outputs_free(t)
                if n == 0:
                    if j == 0:
                        moments(x_in, t)
                    else:
                        outputs_free(t)
                        scaled(hn, x_in, t).then_inc(st["pre_done"].sem, 1)
                elif n == 2:
                    if j == 0:
                        divide(a[:, k, :], t)
                        v.tensor_scalar(e[:, k, :], a[:, k, :], 0.0, None, ALU.min).then_inc(st["exp_in"].sem, 1)
                    else:
                        dve.wait_ge(*st["exp_out"].at(t.no + 1))
                        v.scalar_tensor_tensor(h[:, k, :], a[:, k, :], 0.0, e[:, k, :], ALU.max, ALU.add).then_inc(
                            st["pre_done"].sem, 1)
                elif j == 1:
                    scaled(hn, xn, t).then_inc(st["pre_done"].sem, 1)
                elif n == 3:
                    v.scalar_tensor_tensor(xn, sums(t)[:, 0:DIM], node(0, t), x_in, ALU.mult, ALU.add)
                    v.drain()
                    moments(xn, t)
                elif n == 4:
                    hp = tin["h"][:, k, :]
                    v.scalar_tensor_tensor(at_, sums(t)[:, 0:DIM], node(0, t), tin["hs"][:, k, :], ALU.mult, ALU.add)
                    v.tensor_scalar(hp, hp, 0.0, None, ALU.max)
                    v.drain()
                    v.tensor_scalar(at_, at_, node(2, t), None, ALU.mult)
                    v.tensor_tensor(x_in, x_in, hp, ALU.add)
                    v.drain()
                    v.scalar_tensor_tensor(at_, hp, node(3, t), at_, ALU.mult, ALU.add)
                    v.drain()
                    v.scalar_tensor_tensor(xn, at_, 0.0, x_in, ALU.max, ALU.add)
                    v.drain()
                    moments(xn, t)
                elif n == 5:
                    join_self(t)
                    v.tensor_scalar(b[:, k, :], a[:, k, :], 0.0, vec1[:, 0:1], ALU.min, ALU.mult)
                    v.drain()
                    v.scalar_tensor_tensor(h[:, k, :], a[:, k, :], 0.0, b[:, k, :], ALU.max, ALU.add).then_inc(
                        st["pre_done"].sem, 1)
                elif n == 6:
                    join_self(t)
                    v.tensor_tensor(xn, at_, x_in, ALU.add).then_inc(st["pre_done"].sem, 1)

            def slot_of_four(t0, t1, t2, t3):
                def of(t):
                    k = t.b
                    return a[:, k, 0:DIM], b[:, k, 0:DIM], e[:, k, 0:DIM], xo[:, k, :], h[:, k, 0:DIM]

                if t2:
                    at_, bt, et, xn, _ = of(t2)
                    dve.wait_ge(*st["exp_out"].at(t2.no + 1))
                    v.scalar_tensor_tensor(bt, et, -1.0, tin["x"][:, t2.b, :], ALU.add, ALU.add)
                if t0:
                    begin(t0)
                    H = prev.heads
                    v.tensor_tensor(per_head(a[:, t0.b, 0:DIM], H), per_head(sums(t0)[:, 0:DIM], H),
                                    node(0, t0, 0, H).unsqueeze(2).to_broadcast([P, H, prev.depth]), ALU.mult)
                v.drain()
                if t2:
                    outputs_free(t2)
                    v.scalar_tensor_tensor(xn, at_, 0.0, bt, ALU.max, ALU.add)
                if t0:
                    v.scalar_tensor_tensor(a[:, t0.b, 0:DIM], tin["h"][:, t0.b, :], 0.0, a[:, t0.b, 0:DIM],
                                           ALU.max, ALU.add)
                if t3:
                    scaled(of(t3)[4], of(t3)[3], t3, 1).then_inc(st["pre_done"].sem, 1)
                if t1:
                    dve.wait_ge(*st["inv_std0"].at(t1.no + 1))
                    v.scalar_tensor_tensor(of(t1)[1], of(t1)[0], small[:, t1.b, 6:7], vec[:, 0, 0:DIM],
                                           ALU.subtract, ALU.mult)
                v.drain()
                if t1:
                    v.scalar_tensor_tensor(of(t1)[0], of(t1)[1], small[:, t1.b, 9:10], vec[:, 1, 0:DIM],
                                           ALU.mult, ALU.add).then_inc(st["exp_in"].sem, 1)
                if t2:
                    v.bn_stats(small[:, t2.b, 0:6], xn)
                if t0:
                    v.bn_stats(small[:, t0.b, 0:6], a[:, t0.b, 0:DIM])
                v.drain()
                if t2:
                    v.bn_aggr(small[:, t2.b, 6:8], small[:, t2.b, 0:6]).then_inc(st["variance1"].sem, 1)
                if t0:
                    v.bn_aggr(small[:, t0.b, 6:8], small[:, t0.b, 0:6]).then_inc(st["variance0"].sem, 1)

            if prev:
                factors()
            if joined:
                weights()

            def slot(behind):
                if n == 1:
                    slot_of_four(behind(0), behind(1), behind(2), behind(3))
                else:
                    for j in range(last + 1):
                        t = behind(j)
                        if t:
                            stage(j, t)
                t = behind(0)
                if t and t.known and t.no == 0 and not joined:
                    weights()

            slots_of_nodes(slot, dve, n)

        if norms:
            @blk.gpsimd
            def _(pool):
                def slot(behind):
                    for which in range(len(norms) - 1, -1, -1):
                        t = behind(norms[which])
                        if t:
                            pool.wait_ge(*st[f"variance{which}"].at(t.no + 1))
                            nc.gpsimd.tensor_tensor(small[:, t.b, 8:9], small[:, t.b, 7:8], sb["eps"][:, :], ALU.add)
                            nc.gpsimd.drain()
                            nc.gpsimd.tensor_tensor(small[:, t.b, 9:10], small[:, t.b, 8:9], sb["minus_half"][:, :],
                                                    ALU.pow).then_inc(st[f"inv_std{which}"].sem, 1)

                slots_of_nodes(slot, pool, n)

        @blk.scalar
        def _(act):
            if joined:
                act.wait_ge(*st["exp_in"].at(1))
                nc.scalar.activation(per_node[:, 6:8, :], per_node[:, 6:8, :], ACT.Exp).then_inc(
                    st["exp_out"].sem, 1)

            def slot(behind):
                t = behind(EXP_STAGE[n]) if n in EXP_STAGE else None
                if t:
                    wide = 512 if n == 2 else DIM
                    et = e[:, t.b, 0:wide]
                    act.wait_ge(*st["exp_in"].at(t.no + 1))
                    if n == 1:
                        nc.scalar.activation(et, a[:, t.b, 0:wide], ACT.Relu, scale=-1.0)
                        nc.scalar.drain()
                    m = nc.scalar.activation(et, et, ACT.Exp, scale=-1.0 if n == 1 else 1.0)
                    if n == 2:
                        nc.scalar.drain()
                        m = nc.scalar.activation(et, et, ACT.Copy, bias=-1.0)
                    m.then_inc(st["exp_out"].sem, 1)
                t = behind(last)
                if t and L:
                    if t.first >= NODE_RING:
                        act.wait_ge(*st["proj_ps"].at(t.no - NODE_RING + 1))
                    act.wait_ge(*st["hT_ps"].at(t.no + 1))
                    nc.scalar.activation(hT[:, t.b, 0:L.k], psum_t[t.b][:, 0:L.k],
                                         ACT.Relu if norms else ACT.Copy).then_inc(st["hT_sb"].sem, 1)
                t = behind(last + 2)
                if t and L:
                    if t.reused:
                        act.wait_ge(*st[f"tb{t.b}"].at(16 * tb_stores * t.turn))
                    act.wait_ge(*st["proj_ps"].at(t.no + 1))
                    F, H = L.feat, L.heads
                    ps = psum_f[t.b % 2]
                    nc.scalar.activation(tb[:, t.b, 0:L.row], ps[:, 0:L.row], ACT.Copy)
                    if L.extra:
                        nc.scalar.activation(tb[:, t.b, L.row:], ps[:, 512:512 + L.extra], ACT.Copy)
                    if L.self_loop:
                        nc.scalar.activation(sb["el_own"][:, bass.ds(t.no * H, H)], ps[:, F:F + H], ACT.Copy)
                    nc.scalar.activation(sb["er"][:, bass.ds(t.no * H, H)], ps[:, F + H:F + 2 * H],
                                         ACT.Copy).then_inc(st["table_sb"].sem, 1)

            if L or joined:
                slots_of_nodes(slot, act, n)

        if L:
            @blk.tensor
            def _(pe):
                def slot(behind):
                    t = behind(last)
                    if t:
                        if t.first >= NODE_RING:
                            pe.wait_ge(*st["hT_sb"].at(t.no - NODE_RING + 1))
                        pe.wait_ge(*st["pre_done"].at(t.no + 1))
                        for k in range(L.chunks):
                            mm = nc.tensor.transpose(psum_t[t.b][:, k * P:(k + 1) * P],
                                                     h[:, t.b, k * P:(k + 1) * P], sb["ident"][:, :])
                        mm.then_inc(st["hT_ps"].sem, 1)
                    t = behind(last + 1)
                    if t:
                        if t.known and t.no == 0:
                            pe.wait_ge(*st["w_ready"].at(1))
                        if t.first >= 2:
                            pe.wait_ge(*st["table_sb"].at(t.no - 2 + 1))
                        pe.wait_ge(*st["hT_sb"].at(t.no + 1))
                        for lo, hi, at in ((0, split, 0), (split, L.proj, 512)):
                            for k in range(L.chunks):
                                if lo < hi:
                                    mm = nc.tensor.matmul(psum_f[t.b % 2][:, at:at + hi - lo],
                                                          hT[:, t.b, k * P:(k + 1) * P], wx[:, k, lo:hi],
                                                          start=(k == 0), stop=(k == L.chunks - 1))
                        mm.then_inc(st["proj_ps"].sem, 1)

                slots_of_nodes(slot, pe, n)

    if L:
        for name in ("hT_ps", "hT_sb", "proj_ps", "table_sb"):
            st[name].base += BLOCKS
        st["w_ready"].base += 1
    for which in range(len(norms)):
        st[f"variance{which}"].base += BLOCKS
        st[f"inv_std{which}"].base += BLOCKS
    st["w_in"].base += 16 * len(w_loads)
    st["pre_done"].base += BLOCKS
    for name in ("exp_in", "exp_out"):
        st[name].base += 1 if joined else BLOCKS if n in EXP_STAGE else 0
    for k in range(NODE_RING):
        tiles = (BLOCKS + NODE_RING - 1 - k) // NODE_RING
        st[f"in{k}"].base += 16 * len(loads) * tiles
        st[f"out{k}"].base += 16 * len(stores) * tiles
        st[f"tb{k}"].base += 16 * tb_stores * tiles


def edge_pass(nc, st, io, sb, n):
    L = LAYERS[n]
    H, D, F = L.heads, L.depth, L.feat
    CW = L.acc
    HALF = CW // 2 if CW > 512 else CW
    GE = GROUP * P
    wide = CW > 512
    ring = 3 if wide else MAX_RING
    sum_bufs = 2 if wide else 4
    act_steps = ACT_STEPS[n]
    dve_steps = [s for s in range(GROUP) if s not in act_steps]
    with ExitStack() as c:
        def tmp(name, shape, dt=F32):
            return c.enter_context(nc.sbuf_tensor(f"e{n}_{name}", shape, dt))

        rows = [tmp(f"rows{r}", [P, GROUP, CW]) for r in range(ring)]
        idx = tmp("idx", [P, ring, GROUP], I32)
        bytes_in = tmp("bytes_in", [P, 2, GE], U8)
        onehot = tmp("onehot", [P, 2, GROUP, P])
        onehot_T = tmp("onehot_T", [P, GROUP, P], BF16)
        er_parts = tmp("er_parts", [P, BLOCKS * H, 3], BF16)
        er_rest = tmp("er_rest", [P, BLOCKS * H])
        er_edge = tmp("er_edge", [P, 2, GROUP, H])
        el = tmp("el", [P, 2, GROUP, H])
        pens = tmp("pens", [MAX_HEADS, 2, 2, GE], BF16)
        forward = tmp("forward", [MAX_HEADS, GE])
        top = tmp("top", [MAX_HEADS, GE + P])
        logit = tmp("logit", [P, 2 * GROUP + 1, H])
        diff = tmp("diff", [P, GROUP, H])
        drop = tmp("drop", [P, H])
        rho = tmp("rho", [P, H])
        ps_el = c.enter_context(nc.psum_tensor(f"e{n}_ps_el", [P, GE], F32))
        ps_sum = [c.enter_context(nc.psum_tensor(f"e{n}_ps_sum{b}", [P, 2048 // sum_bufs], F32))
                  for b in range(sum_bufs)]
        ps_er_all = c.enter_context(nc.psum_tensor(f"e{n}_ps_er", [P, 512], F32))
        ps_small = c.enter_context(nc.psum_tensor(f"e{n}_ps_small", [P, 512], F32))
        ps_er = ps_er_all[:, 0:GROUP * 3 * H].rearrange("p (s h c) -> p s h c", h=H, c=3)
        ps_top = ps_small[:, 0:(GROUP + 1) * H].rearrange("p (s h) -> p s h", h=H)
        ps_rho = ps_small[:, 256:256 + H]
        blk = c.enter_context(nc.Block())


        def blocks_of(kind, g):
            _, got = nc.values_load_multi_w_load_instructions(
                sb["block_of"][0:1, bass.ds(g * GROUP_UNITS, GROUP_UNITS)], engines=(kind,), min_val=0,
                max_val=BLOCKS - 1, skip_runtime_bounds_check_because="the walk's blocks are clamped")
            return got

        @blk.sync
        def _(sp):
            def slot(c):
                if not c.within(0):
                    return
                g, p = c.no, c.p
                sp.wait_ge(*st["scanned"].at(g - 1))
                src = io["pen"][:, bass.ds(g * GE, GE)].unsqueeze(0).to_broadcast([H, 2, GE])
                sp.dma_start(pens[0:H, p, :, :], src).then_inc(st[f"pens{p}"].sem, 16)
                sp.wait_ge(*st["onehot"].at(g - 1))
                sp.dma_start(bytes_in[:, p, :], io["onehot"][bass.ds(g * P, P), :]).then_inc(
                    st[f"bytes{p}"].sem, 16)

            slots_of_pass(slot, sp, ring)

        @blk.gpsimd
        def _(pool):
            def slot(c):
                if not c.within(0):
                    return
                g, r = c.no, c.r
                pool.wait_ge(*st["idx_ready"].at(g + 1))
                for s in range(GROUP):
                    if s % UNIT == 0:
                        if c.at_least(ring):
                            pool.wait_ge(*st["summed"].at(GROUP_UNITS * (g - ring) + s // UNIT + 1))
                        pool.sem_inc(st["gathering"].sem, 1)
                    nc.gpsimd.indirect_dma_start(
                        out=rows[r][:, s, 0:L.row], out_offset=None, in_=io[f"rows{n}"][:, :],
                        in_offset=bass.IndirectOffsetOnAxis(ap=idx[:, r, s:s + 1], axis=0)).then_inc(
                            st[f"rows{r}"].sem, 16)

            slots_of_pass(slot, pool, ring)

        @blk.vector
        def _(dve):
            v = nc.vector

            def indices(g, r):
                v.tensor_copy(idx[:, r, :], sb["src_of"][:, bass.ds(g * GROUP, GROUP)]).then_inc(
                    st["idx_ready"].sem, 1)

            def split_er():
                for part in range(3):
                    src = sb["er"][:, 0:BLOCKS * H] if part == 0 else er_rest[:, :]
                    v.tensor_copy(er_parts[:, :, part], src)
                    v.drain()
                    if part < 2:
                        v.tensor_tensor(er_rest[:, :], src, er_parts[:, :, part], ALU.subtract)
                        v.drain()
                v.drain().then_inc(st["er_parts"].sem, 1)

            def source_logits(c, ahead):
                g, p, r = c.no + ahead, (c.p + ahead) % 2, (c.r + ahead) % ring
                dve.wait_ge(*st[f"rows{r}"].at(16 * GROUP * (c.turn(ahead) + 1)))
                if L.edge_term:
                    v.tensor_tensor(el[:, p, :, 0], rows[r][:, :, F], sb["edge_term"][:, bass.ds(g * GROUP, GROUP)],
                                    ALU.add).then_inc(st["el"].sem, 1)
                else:
                    v.tensor_copy(el[:, p, :, :], rows[r][:, :, F:F + H]).then_inc(st["el"].sem, 1)
                indices(g + ring, r)

            def destination_logits(c, ahead):
                dve.wait_ge(*st["er_ps"].at(c.no + ahead + 1))
                v.tensor_reduce(er_edge[:, (c.p + ahead) % 2, :, :], ps_er, AX_X, ALU.add).then_inc(
                    st["er_sb"].sem, 1)

            def scans(c):
                g, p = c.no, c.p
                dve.wait_ge(*st[f"pens{p}"].at(16 * (c.half + 1)))
                dve.wait_ge(*st["el_ps"].at(g + 1))
                v.tensor_tensor_scan(forward[0:H, :], pens[0:H, p, 0, :], ps_el[0:H, :], sb["carry"][0:H, 0:1],
                                     ALU.add, ALU.max)
                v.tensor_scalar(top[0:H, GE:GE + P], sb["ones"][0:H, :], sb["carry"][0:H, 0:1], None, ALU.mult)
                v.drain()
                v.tensor_tensor_scan(top[0:H, GE - 1::-1], pens[0:H, p, 1, ::-1], forward[0:H, ::-1], LOW,
                                     ALU.add, ALU.max)
                v.tensor_copy(sb["carry"][0:H, 0:1], forward[0:H, GE - 1:GE]).then_inc(st["scanned"].sem, 1)

            def exponents(u, q, r):
                dve.wait_ge(*st["top_ps"].at(u + 1))
                v.tensor_tensor(logit[:, GROUP:2 * GROUP, :], ps_top[:, 0:GROUP, :], er_edge[:, q, :, :], ALU.add)
                v.tensor_tensor(logit[:, 2 * GROUP, :], ps_top[:, GROUP, :], er_edge[:, q, 0, :], ALU.add)
                v.tensor_tensor(logit[:, 0:GROUP, :], el[:, q, :, :], er_edge[:, q, :, :], ALU.add)
                if L.self_loop:
                    v.tensor_tensor(rows[r][:, :, F + H:F + 2 * H], ps_top[:, 0:GROUP, :],
                                    sb["ends_here"][:, bass.ds(u * GROUP, GROUP)].unsqueeze(2).to_broadcast(
                                        [P, GROUP, H]), ALU.mult)
                v.drain()
                v.scalar_tensor_tensor(logit[:, :, :], logit[:, :, :], L.slope, logit[:, :, :], ALU.mult, ALU.max)
                v.drain()
                v.tensor_tensor(diff[:, :, :], logit[:, 0:GROUP, :], logit[:, GROUP:2 * GROUP, :],
                                ALU.subtract).then_inc(st["diff"].sem, 1)
                v.tensor_tensor(drop[:, :], logit[:, 2 * GROUP, :], logit[:, GROUP, :], ALU.subtract)
                v.drain()
                v.tensor_scalar(drop[:, :], drop[:, :], sb["goes_on"][:, bass.ds(u, 1)], None, ALU.mult).then_inc(
                    st["exponents"].sem, 1)

            def messages(u, r, k):
                R = rows[r]
                for s in range(UNIT * k, UNIT * (k + 1)):
                    if s in dve_steps:
                        dve.wait_ge(*st["weights"].at(u + 1))
                        v.tensor_tensor(per_head(R[:, s, 0:F], H), per_head(R[:, s, 0:F], H),
                                        R[:, s, F:F + H].unsqueeze(2).to_broadcast([P, H, D]), ALU.mult).then_inc(
                                            st["message"].sem, 1)

            def rescale(u, block):
                dve.wait_ge(*st["rho"].at(u + 1))
                if not (isinstance(u, int) and u == 0):
                    dve.wait_ge(*st["added"].at(GROUP_UNITS * u))
                A = sb["acc"][:, bass.ds(block * CW, CW)]
                v.tensor_tensor(per_head(A[:, 0:F], H), per_head(A[:, 0:F], H),
                                rho[:, :].unsqueeze(2).to_broadcast([P, H, D]), ALU.mult)
                v.tensor_tensor(A[:, F:F + H], A[:, F:F + H], rho[:, :], ALU.mult)
                v.drain()

            def add(u, k, block):
                dve.wait_ge(*st["added"].at(GROUP_UNITS * u + k))
                dve.wait_ge(*st["summed"].at(GROUP_UNITS * u + k + 1))
                A = sb["acc"][:, bass.ds(block * CW, CW)].rearrange("p (j c) -> p j c", c=HALF)
                S = ps_sum[k % sum_bufs][:, :].rearrange("p (j c) -> p j c", c=512)[:, 0:CW // HALF, 0:HALF]
                v.tensor_tensor(A, A, S, ALU.add).then_inc(st["added"].sem, 1)

            def slot(c):
                g, u, r = c.no, c.no - 1, (c.r - 1) % ring
                last_unit = GROUP_UNITS - 1
                if not c.at_least(1):
                    for j in range(ring):
                        indices(j, j)
                    split_er()
                    v.memset(sb["carry"][:, :], 0.0)
                    v.memset(sb["acc"][:, 0:BLOCKS * CW], 0.0)
                    source_logits(c, 0)
                    destination_logits(c, 0)
                if c.at_least(1):
                    messages(u, r, 0)
                if c.within(0):
                    scans(c)
                if c.within(1) and not wide:
                    source_logits(c, 1)
                if c.at_least(1):
                    messages(u, r, 1)
                if c.at_least(2):
                    add(g - 2, last_unit, blocks_of(mybir.EngineType.DVE, g - 2)[last_unit])
                if c.at_least(1):
                    blocks = blocks_of(mybir.EngineType.DVE, u)
                    rescale(u, blocks[0])
                    if wide:
                        messages(u, r, 2)
                    add(u, 0, blocks[0])
                if c.within(1):
                    destination_logits(c, 1)
                if c.at_least(1):
                    if not wide:
                        messages(u, r, 2)
                    messages(u, r, 3)
                if c.within(1) and wide:
                    source_logits(c, 1)
                if c.at_least(1) and wide:
                    add(u, 1, blocks[1])
                if c.within(0):
                    exponents(g, c.p, c.r)
                if c.at_least(1):
                    if not wide:
                        add(u, 1, blocks[1])
                    add(u, 2, blocks[2])
                if not c.within(0):
                    add(u, last_unit, blocks[last_unit])

            slots_of_pass(slot, dve, ring)

        @blk.tensor
        def _(pe):
            ident = sb["ident"]

            def turn_source_logits(c, ahead):
                g, p = c.no + ahead, (c.p + ahead) % 2
                pe.wait_ge(*st["scanned"].at(g))
                pe.wait_ge(*st["el"].at(g + 1))
                for s in range(GROUP):
                    mm = nc.tensor.transpose(ps_el[0:H, s * P:(s + 1) * P], el[:, p, s, :], ident[:, :])
                mm.then_inc(st["el_ps"].sem, 1)

            def pick_destination_logits(c, ahead):
                g = c.no + ahead
                blocks = blocks_of(mybir.EngineType.PE, g)
                pe.wait_ge(*st["er_sb"].at(g))
                pe.wait_ge(*st["turned_sb"].at(g + 1))
                for s in range(GROUP):
                    mm = nc.tensor.matmul(
                        ps_er[:, s, :, :].rearrange("p h c -> p (h c)"), onehot_T[:, s, :],
                        er_parts[:, bass.ds(blocks[s // UNIT] * H, H), :].rearrange("p h c -> p (h c)"),
                        start=True, stop=True)
                mm.then_inc(st["er_ps"].sem, 1)

            def slot(c):
                g = c.no
                u, q, r = g - 1, 1 - c.p, (c.r - 1) % ring

                def sums(k):
                    pe.wait_ge(*st["added"].at(GROUP_UNITS * u + k + 1 - sum_bufs))
                    for j in range(UNIT):
                        s = UNIT * k + j
                        if s in dve_steps:
                            pe.wait_ge(*st["message"].at(len(dve_steps) * u + dve_steps.index(s) + 1))
                        else:
                            pe.wait_ge(*st["message_act"].at(len(act_steps) * u + act_steps.index(s) + 1))
                        for h in range(CW // HALF):
                            mm = nc.tensor.matmul(ps_sum[k % sum_bufs][:, 512 * h:512 * h + HALF],
                                                  onehot[:, q, s, :], rows[r][:, s, HALF * h:HALF * (h + 1)],
                                                  start=(j == 0), stop=(j == UNIT - 1))
                    mm.then_inc(st["summed"].sem, 1)

                if not c.at_least(1):
                    pe.wait_ge(*st["er_parts"].at(1))
                    turn_source_logits(c, 0)
                    pick_destination_logits(c, 0)
                else:
                    pe.wait_ge(*st["onehot"].at(g))
                    pe.wait_ge(*st["exponents"].at(g))
                    nc.tensor.matmul(ps_rho, onehot[:, q, 0, :], drop[:, :], start=True, stop=True).then_inc(
                        st["rho_ps"].sem, 1)
                    sums(0)
                if c.within(1):
                    pick_destination_logits(c, 1)
                if c.within(0):
                    pe.wait_ge(*st["rho"].at(g))
                    pe.wait_ge(*st["scanned"].at(g + 1))
                    nc.tensor.matmul(ps_top[:, 0, :], top[0:H, 0:P], ident[0:H, 0:H], start=True, stop=True)
                    for s in range(1, GROUP + 1):
                        mm = nc.tensor.transpose(ps_top[:, s, :], top[0:H, s * P:(s + 1) * P], ident[0:H, 0:H])
                    mm.then_inc(st["top_ps"].sem, 1)
                if c.within(1) and not wide:
                    turn_source_logits(c, 1)
                if c.at_least(1):
                    sums(1)
                    sums(2)
                if c.within(1) and wide:
                    turn_source_logits(c, 1)
                if c.at_least(1):
                    sums(3)

            slots_of_pass(slot, pe, ring)

        @blk.scalar
        def _(act):
            def turned(g):
                act.wait_ge(*st["er_ps"].at(g))
                nc.scalar.activation(onehot_T[:, :, :].rearrange("p s e -> p (s e)"),
                                     sb["onehot_T"][:, bass.ds(g * GE, GE)], ACT.Copy).then_inc(
                                         st["turned_sb"].sem, 1)

            def slot(c):
                g, p = c.no, c.p
                u, r = g - 1, (c.r - 1) % ring
                R = rows[r]
                if c.at_least(1):
                    act.wait_ge(*st["diff"].at(g))
                    nc.scalar.activation(R[:, :, F:F + H], diff[:, :, :], ACT.Exp).then_inc(st["weights"].sem, 1)
                    act.wait_ge(*st["weights"].at(g))
                    for s in act_steps:
                        for h in range(H):
                            m = nc.scalar.activation(R[:, s, h * D:(h + 1) * D], R[:, s, h * D:(h + 1) * D],
                                                     ACT.Copy, scale=R[:, s, F + h:F + h + 1])
                        m.then_inc(st["message_act"].sem, 1)
                        if s == act_steps[0]:
                            act.wait_ge(*st["rho_ps"].at(g))
                            nc.scalar.activation(rho[:, :], ps_rho, ACT.Exp).then_inc(st["rho"].sem, 1)
                else:
                    turned(0)
                    turned(1)
                if c.within(0):
                    act.wait_ge(*st["summed"].at(GROUP_UNITS * (g - 1)))
                    act.wait_ge(*st[f"bytes{p}"].at(16 * (c.half + 1)))
                    nc.scalar.activation(onehot[:, p, :, :].rearrange("p s d -> p (s d)"), bytes_in[:, p, :],
                                         ACT.Copy).then_inc(st["onehot"].sem, 1)
                if c.within(2):
                    turned(g + 2)

            slots_of_pass(slot, act, ring)

    for name in ("scanned", "idx_ready", "onehot", "el", "el_ps", "er_ps", "er_sb", "top_ps",
                 "exponents", "diff", "weights", "rho", "rho_ps", "turned_sb"):
        st[name].base += GROUPS
    st["idx_ready"].base += ring
    st["er_parts"].base += 1
    st["gathering"].base += GROUPS * GROUP_UNITS
    for name in ("summed", "added"):
        st[name].base += GROUPS * GROUP_UNITS
    st["message"].base += GROUPS * len(dve_steps)
    st["message_act"].base += GROUPS * len(act_steps)
    for p in range(2):
        st[f"pens{p}"].base += 16 * ((GROUPS + 1 - p) // 2)
        st[f"bytes{p}"].base += 16 * ((GROUPS + 1 - p) // 2)
    for r in range(ring):
        st[f"rows{r}"].base += 16 * GROUP * ((GROUPS + ring - 1 - r) // ring)


STAGES = [
    "variance0", "variance1", "inv_std0", "inv_std1", "w_in", "w_ready", "pre_done", "exp_in", "exp_out",
    "hT_ps", "hT_sb", "proj_ps", "table_sb",
    *(f"{name}{k}" for name in ("in", "out", "tb") for k in range(NODE_RING)),
    "scanned", "idx_ready", "onehot", "el", "el_ps", "er_ps", "er_sb", "top_ps", "exponents", "weights", "rho",
    "rho_ps", "turned_sb", "er_parts", "oh_used", "oh_flat", "diff", "oh_in0", "oh_in1", "oh_out0", "oh_out1",
    "bytes0", "bytes1", "message", "summed", "added", "pens0", "pens1", "rows0", "rows1", "rows2", "rows3",
    "message_act", "gathering",
]


def build(nc, io):
    with ExitStack() as ctx:
        def keep(name, shape, dt=F32):
            return ctx.enter_context(nc.sbuf_tensor(name, shape, dt))

        sb = {
            "acc": keep("acc", [P, BLOCKS * MAX_ACC]),
            "er": keep("er", [P, BLOCKS * MAX_HEADS]),
            "src_of": keep("src_of", [P, STEPS + MAX_RING * GROUP], I32),
            "dst_in_block": keep("dst_in_block", [P, STEPS]),
            "ends_here": keep("ends_here", [P, STEPS]),
            "edge_term": keep("edge_term", [P, STEPS]),
            "goes_on": keep("goes_on", [P, GROUPS]),
            "block_of": keep("block_of", [P, WALK], I32),
            "onehot_T": keep("onehot_nodes", [P, STEPS * P], U8),
            "lane": keep("lane", [P, 1]),
            "ident": keep("ident", [P, P]),
            "iota": keep("iota", [P, P]),
            "ones": keep("ones", [P, P]),
            "carry": keep("carry", [P, 1]),
            "minus_half": keep("minus_half", [P, 1]),
            "eps": keep("eps", [P, 1]),
            "el_own": keep("el_own", [P, BLOCKS * 4]),
        }
        st = {name: Stage(nc, ctx, name) for name in STAGES}

        def scratch(name, shape, dt=F32):
            return nc.dram_tensor("dram_" + name, shape, dt, kind="Internal").ap()

        NP = BLOCKS * P
        io["walk_rows"] = scratch("walk_rows", [WALK_ROWS * P * UE + 2 * P], I32)
        io["walk_block"] = scratch("walk_block", [WALK_ROWS * P], I32)
        io["ea_flat"] = scratch("ea_flat", [P, UNITS * UNIT])
        io["ea_units"] = io["ea_flat"].rearrange("p j -> (p j)").rearrange("(t q) -> t q", q=UE)
        io["dst_local"] = scratch("dst_local", [WALK_ROWS * P * UE], BF16)
        io["pen"] = scratch("pen", [2, WALK_ROWS * P * UE], BF16)
        io["onehot"] = scratch("onehot", [GROUPS * P, GROUP * P], U8)
        io["x_mid"] = scratch("x_mid", [NP, DIM])
        io["h_mid"] = scratch("h_mid", [NP, DIM])
        io["hs_mid"] = scratch("hs_mid", [NP, DIM])
        for n, L in enumerate(LAYERS):
            io[f"rows{n}"] = scratch(f"rows_table{n}", [NP, L.row])

        with nc.Block() as blk:
            @blk.vector
            def _(dve):
                nc.vector.memset(sb["ones"][:, :], 1.0)
                nc.vector.memset(sb["minus_half"][:, :], -0.5)
                nc.vector.memset(sb["eps"][:, :], LN_EPS)
                nc.vector.memset(sb["src_of"][:, STEPS:], 0)
        prepare(nc, ctx, st, io, {**sb, "src_of": sb["src_of"][:, 0:STEPS]})
        make_onehots(nc, st, io, sb)
        for n in range(len(LAYERS) + 1):
            node_phase(nc, st, io, sb, n)
            if n < len(LAYERS):
                edge_pass(nc, st, io, sb, n)


def kernel(**inputs):
    import numpy as np
    import concourse.bacc as bacc
    from concourse import mybir as mb
    from concourse.bass_utils import run_bass_kernel_spmd as run

    x = {k: np.asarray(v) for k, v in inputs.items()}
    NP, EP = BLOCKS * P, UNITS * UE

    def pad(a, rows, fill):
        out = np.full((rows,) + a.shape[1:], fill, a.dtype)
        out[:a.shape[0]] = a
        return out

    dst = pad(x["dst"], EP, NO_NODE)
    arrays = {
        "x": pad(x["x"], NP, 0),
        "src_units": pad(x["src"], EP, 0).reshape(UNITS, UE),
        "dst_units": dst.reshape(UNITS, UE),
        "dst_last": dst.reshape(UNITS, UE)[:UNITS - 1, UE - 1],
        "edge_attr": pad(x["edge_attr_64"], EP, 0).reshape(P, UNITS * UNIT * EDGE_DIM),
        "iota": np.arange(512, dtype=np.float32),
        "step_no": np.arange(WALK_ROWS * P, dtype=np.float32).reshape(WALK_ROWS, P).T,
        "ident": np.eye(P, dtype=np.float32),
        "lane": np.arange(P, dtype=np.float32).reshape(P, 1),
        "no_node": np.full((P,), -1, np.int32),
        "att": x["L2_gnn_W_att"].reshape(-1),
        "gamma": x["L0_gnn_gamma"], "beta": x["L0_gnn_beta"],
        "b1": x["L3_gnn_b1"], "b2": x["L3_gnn_b2"], "prelu": x["L3_gnn_prelu_w"].reshape(1),
        "w0": x["L0_gnn_W"], "w1": x["L1_gnn_W1"], "w2": x["L1_gnn_W2"],
        "w3": np.concatenate([x["L2_gnn_W_func"].T, x["L2_gnn_W_self"].T], axis=1),
        "w4": x["L3_gnn_W1"], "w5": x["L3_gnn_W2"],
        "a0": np.stack([x["L0_gnn_a_src"].reshape(-1), x["L0_gnn_a_dst"].reshape(-1)]),
        "a1": np.stack([x["L1_gnn_attn_l1"].reshape(-1), x["L1_gnn_attn_r1"].reshape(-1)]),
        "a2": np.stack([x["L1_gnn_attn_l2"].reshape(-1), x["L1_gnn_attn_r2"].reshape(-1)]),
        "a3": x["L2_gnn_W_att"].reshape(-1)[:2 * DIM].reshape(2, DIM),
        "a4": np.stack([x["L3_gnn_a_src1"].reshape(-1), x["L3_gnn_a_dst1"].reshape(-1)]),
        "a5": np.stack([x["L3_gnn_a_src2"].reshape(-1), x["L3_gnn_a_dst2"].reshape(-1)]),
    }
    arrays = {"in_" + k: np.ascontiguousarray(v) for k, v in arrays.items()}
    nc = bacc.Bacc("TRN2", target_bir_lowering=False, num_devices=1)
    io = {k[3:]: nc.dram_tensor(k, v.shape, mb.dt.from_np(v.dtype), kind="ExternalInput").ap()
          for k, v in arrays.items()}
    io["out"] = nc.dram_tensor("out", (NP, DIM), mb.dt.float32, kind="ExternalOutput").ap()
    build(nc, io)
    r = run(nc, [arrays], core_ids=[0])
    return r.results[0]["out"][:NODES]
```
